# Optimizing a Trainium2 kernel written in Bass

```python
import numpy as np
import jax
import jax.numpy as jnp

def _softmax(x, axis=-1):
    return jax.nn.softmax(x, axis=axis)

def _gelu(x):
    return jax.nn.gelu(x, approximate=True)

def _silu(x):
    return jax.nn.silu(x)

def _sigmoid(x):
    return jax.nn.sigmoid(x)

def _layernorm(x, axis=-1, eps=1e-05):
    m = jnp.mean(x, axis=axis, keepdims=True)
    v = jnp.var(x, axis=axis, keepdims=True)
    return (x - m) / jnp.sqrt(v + eps)

def _scatter_add(tgt, idx, src, axis=0):
    return tgt.at[idx].add(src)

def _segment_sum(src, seg, n):
    return jax.ops.segment_sum(src, seg, n)
kernel_name = 'mk_macaron_d1_jaxref_r4_713f3a'

def setup_inputs(seed: int=0):
    np.random.seed(seed)
    _w = jnp.asarray

    def _L0_attn_setup():
        import jax, jax.numpy as jnp
        import numpy as np
        D_MODEL = 256
        NUM_HEADS = 16
        DILATION_RATE = 4
        SEGMENT_SIZE = 128
        BATCH = 4
        SEQ_LEN = 2048

        def _branch(x, Wqkv_i, bqkv_i, Wo_i, bo_i, offset):
            B, S, D = x.shape
            hd = D // NUM_HEADS
            x_ = x[:, offset::DILATION_RATE, :]
            n_seg = x_.shape[1] // SEGMENT_SIZE
            x_ = x_.reshape(B, n_seg, SEGMENT_SIZE, D)
            qkv = jnp.einsum('bnsd,ed->bnse', x_, Wqkv_i) + bqkv_i
            q, k, v = jnp.split(qkv, 3, axis=-1)
            q = q.reshape(B, n_seg, SEGMENT_SIZE, NUM_HEADS, hd)
            k = k.reshape(B, n_seg, SEGMENT_SIZE, NUM_HEADS, hd)
            v = v.reshape(B, n_seg, SEGMENT_SIZE, NUM_HEADS, hd)
            scores = jnp.einsum('bnqhd,bnkhd->bnhqk', q, k) / jnp.sqrt(jnp.asarray(hd, q.dtype))
            attn = jax.nn.softmax(scores, axis=-1)
            o = jnp.einsum('bnhqk,bnkhd->bnqhd', attn, v).reshape(B, n_seg, SEGMENT_SIZE, D)
            o = jnp.einsum('bnsd,ed->bnse', o, Wo_i) + bo_i
            full = jnp.zeros((B, S, D), x.dtype).at[:, offset::DILATION_RATE, :].set(o.reshape(B, -1, D))
            return full
        key = jax.random.key(seed)
        k_x, k_wqkv, k_wo = jax.random.split(key, 3)
        x = jax.random.normal(k_x, (BATCH, SEQ_LEN, D_MODEL), dtype=jnp.float32)
        Wqkv = jax.random.normal(k_wqkv, (DILATION_RATE, 3 * D_MODEL, D_MODEL), dtype=jnp.float32) * 0.02
        bqkv = jnp.zeros((DILATION_RATE, 3 * D_MODEL), dtype=jnp.float32)
        Wo = jax.random.normal(k_wo, (DILATION_RATE, D_MODEL, D_MODEL), dtype=jnp.float32) * 0.02
        bo = jnp.zeros((DILATION_RATE, D_MODEL), dtype=jnp.float32)
        return {'x': x, 'Wqkv': Wqkv, 'bqkv': bqkv, 'Wo': Wo, 'bo': bo}
    _L0_attn_in = _L0_attn_setup()

    def _L0_ffn_setup():
        import jax, jax.numpy as jnp
        import numpy as np
        DM, NEXPERTS, SETS, ESIZE = (256, 32, 4, 32)
        B, S = (2, 2048)
        key = jax.random.key(seed)
        ks = jax.random.split(key, 7)
        sc = 0.02
        return {'x': jax.random.normal(ks[0], (B, S, DM), jnp.float32), 'Wc': jax.random.normal(ks[1], (DM, NEXPERTS, SETS), jnp.float32) * sc, 'bc': jax.random.normal(ks[2], (NEXPERTS, SETS), jnp.float32) * sc, 'W1': jax.random.normal(ks[3], (NEXPERTS, SETS, DM, ESIZE), jnp.float32) * sc, 'b1': jax.random.normal(ks[4], (NEXPERTS, SETS, ESIZE), jnp.float32) * sc, 'W2': jax.random.normal(ks[5], (NEXPERTS, SETS, DM, ESIZE), jnp.float32) * sc, 'b2': jax.random.normal(ks[6], (NEXPERTS, SETS, DM), jnp.float32) * sc}
    _L0_ffn_in = _L0_ffn_setup()
    _d = {'L0_attn_x': _L0_attn_in['x'], 'L0_attn_Wqkv': _L0_attn_in['Wqkv'], 'L0_attn_bqkv': _L0_attn_in['bqkv'], 'L0_attn_Wo': _L0_attn_in['Wo'], 'L0_attn_bo': _L0_attn_in['bo'], 'L0_ffn_Wc': _L0_ffn_in['Wc'], 'L0_ffn_bc': _L0_ffn_in['bc'], 'L0_ffn_W1': _L0_ffn_in['W1'], 'L0_ffn_b1': _L0_ffn_in['b1'], 'L0_ffn_W2': _L0_ffn_in['W2'], 'L0_ffn_b2': _L0_ffn_in['b2']}
    _x0 = _d['L0_attn_x']
    _d['L0_attn_x'] = jax.random.normal(jax.random.fold_in(jax.random.key(seed), 1), (8, 512, 256), dtype=_x0.dtype)
    del _x0
    return _d

def reference(L0_attn_x, L0_attn_Wqkv, L0_attn_bqkv, L0_attn_Wo, L0_attn_bo, L0_ffn_Wc, L0_ffn_bc, L0_ffn_W1, L0_ffn_b1, L0_ffn_W2, L0_ffn_b2):

    def _L0_attn_ref(x, Wqkv, bqkv, Wo, bo):
        import jax, jax.numpy as jnp
        import numpy as np
        D_MODEL = 256
        NUM_HEADS = 16
        DILATION_RATE = 4
        SEGMENT_SIZE = 128
        BATCH = 4
        SEQ_LEN = 2048

        def _branch(x, Wqkv_i, bqkv_i, Wo_i, bo_i, offset):
            B, S, D = x.shape
            hd = D // NUM_HEADS
            x_ = x[:, offset::DILATION_RATE, :]
            n_seg = x_.shape[1] // SEGMENT_SIZE
            x_ = x_.reshape(B, n_seg, SEGMENT_SIZE, D)
            qkv = jnp.einsum('bnsd,ed->bnse', x_, Wqkv_i) + bqkv_i
            q, k, v = jnp.split(qkv, 3, axis=-1)
            q = q.reshape(B, n_seg, SEGMENT_SIZE, NUM_HEADS, hd)
            k = k.reshape(B, n_seg, SEGMENT_SIZE, NUM_HEADS, hd)
            v = v.reshape(B, n_seg, SEGMENT_SIZE, NUM_HEADS, hd)
            scores = jnp.einsum('bnqhd,bnkhd->bnhqk', q, k) / jnp.sqrt(jnp.asarray(hd, q.dtype))
            attn = jax.nn.softmax(scores, axis=-1)
            o = jnp.einsum('bnhqk,bnkhd->bnqhd', attn, v).reshape(B, n_seg, SEGMENT_SIZE, D)
            o = jnp.einsum('bnsd,ed->bnse', o, Wo_i) + bo_i
            full = jnp.zeros((B, S, D), x.dtype).at[:, offset::DILATION_RATE, :].set(o.reshape(B, -1, D))
            return full
        outs = [_branch(x, Wqkv[i], bqkv[i], Wo[i], bo[i], offset=i % DILATION_RATE) for i in range(DILATION_RATE)]
        weights = jax.nn.softmax(jnp.full((DILATION_RATE,), 1.0 / DILATION_RATE, dtype=x.dtype))
        out = outs[0] * weights[0]
        for i in range(1, DILATION_RATE):
            out = out + weights[i] * outs[i]
        return out

    def _L0_ffn_ref(x, Wc, bc, W1, b1, W2, b2):
        import jax, jax.numpy as jnp
        import numpy as np
        DM, NEXPERTS, SETS, ESIZE = (256, 32, 4, 32)
        B, S = (2, 2048)
        b, s, d = x.shape
        g = Wc.shape[1]
        grouped = x.reshape(b, s // g, g, d)
        logits = jnp.einsum('bntd,des->bntes', grouped, Wc) + bc
        tie = jnp.linspace(0.0, 1e-06, g, dtype=x.dtype).reshape(-1, 1, 1)
        logits = logits + tie
        perm = (logits == jnp.max(logits, axis=-3, keepdims=True)).astype(x.dtype)
        permuted = jnp.einsum('bntd,bntes->bnesd', grouped, perm)
        inner = jax.nn.relu(jnp.einsum('bnesd,esdf->bnesf', permuted, W1) + b1)
        result_permuted = jnp.einsum('bnesf,esdf->bnesd', inner, W2) + b2
        result = jnp.einsum('bnesd,bntes->bntd', result_permuted, perm)
        return result.reshape(b, s, d)
    x = L0_attn_x
    x = x + 0.5 * _L0_ffn_ref(_layernorm(x, axis=-1), L0_ffn_Wc, L0_ffn_bc, L0_ffn_W1, L0_ffn_b1, L0_ffn_W2, L0_ffn_b2)
    x = x + _L0_attn_ref(_layernorm(x, axis=-1), L0_attn_Wqkv, L0_attn_bqkv, L0_attn_Wo, L0_attn_bo)
    x = x + 0.5 * _L0_ffn_ref(_layernorm(x, axis=-1), L0_ffn_Wc, L0_ffn_bc, L0_ffn_W1, L0_ffn_b1, L0_ffn_W2, L0_ffn_b2)
    return x

_drawn_inputs = setup_inputs


def setup_inputs(seed=0):
    import zlib

    import numpy as np

    out = dict(_drawn_inputs(seed))
    spreads = {'L0_attn_bqkv': (0.0, 0.8), 'L0_attn_bo': (0.0, 0.309)}
    factors = {'L0_attn_Wqkv': 8.0, 'L0_attn_Wo': 6.266, 'L0_ffn_b1': 8.0}
    for name, (base, spread) in spreads.items():
        noise = np.random.default_rng([zlib.crc32(name.encode()), seed]).standard_normal(out[name].shape)
        drawn = base * np.exp(spread * noise) if base else spread * noise
        out[name] = jnp.asarray(drawn.astype(out[name].dtype))
    for name, factor in factors.items():
        out[name] = (out[name] * factor).astype(out[name].dtype)
    return out
```

```python
from contextlib import ExitStack

import numpy as np
import concourse.bass as bass
from concourse import mybir
from concourse.alu_op_type import AluOpType as ALU

ACT = mybir.ActivationFunctionType
AX = mybir.AxisListType
F32 = mybir.dt.float32
BF16 = mybir.dt.bfloat16

P = 128
BANK = 512
D = 256
C = D // P
TOK = 4096
NT = TOK // P
GT = 32
NG = TOK // GT
G = P // GT
NX = 128
F = 32
J = P // F
NQ = NX // J
PARTS = 3
IT = 4
NI = NT // IT
GI = 2
EPS = 1e-5
BATCH = 8
DIL = 4
H = 16
HD = D // H
HC = P // HD
HB = 4
NB = H // HB
BRANCH_WEIGHT = 1.0 / DIL
HALF = 4


def done(n):
    return n + 3


def slot_done(k, unit=1):
    return (k + 2) * unit


def prime(eng, *sems, by=2):
    for s in sems:
        eng.sem_inc(s, by)


def pipelined(eng, n, *stages):
    most = max(lag for _, lag in stages)
    ahead = most + most % 2

    def step(m, s, static=True):
        for f, lag in stages:
            if static and not 0 <= 2 * m + s - lag < n:
                continue
            back, odd = divmod(lag, 2)
            if odd:
                f(m - back - 1 + s, 1 - s)
            else:
                f(m - back, s)

    for v in range(ahead):
        step(v // 2, v % 2)
    with eng.Fori(0, (n - ahead) // 2) as k:
        for s in range(2):
            step(k + ahead // 2, s, static=False)
    for v in range(n, n + most):
        step(v // 2, v % 2)


def ffn_stage(nc, tag, src, dst, wts):
    parts_d = nc.dram_tensor(f"parts_{tag}", (PARTS, TOK, D), BF16).ap()
    src_items = src.rearrange("(n t p) d -> n p t d", p=P, t=IT)
    src_tiles = src.rearrange("(t p) d -> t p d", p=P)
    dst_tiles = dst.rearrange("(t p) d -> t p d", p=P)
    parts_items = parts_d.rearrange("k (n t p) d -> k n p t d", p=P, t=IT)
    parts_groups = parts_d.rearrange("k (n g t) d -> k n t g d", g=GI * G, t=GT)

    with ExitStack() as ctx:
        def sb(name, shape, dt=F32):
            return ctx.enter_context(nc.sbuf_tensor(f"{name}_{tag}", shape, dt))

        def sem(name):
            return ctx.enter_context(nc.semaphore(f"{name}_{tag}"))

        def sems(name):
            return [sem(f"{name}{s}_") for s in range(2)]

        PT = sb("PT", [P, C, NX, NG])
        flat = PT[:, :, :, :].rearrange("p c x n -> p (c x n)")
        used = [0]

        def carve(names, *shape, dt=F32):
            n = int(np.prod(shape)) * (2 if dt == BF16 else 4) // 4
            v = flat[:, used[0]:used[0] + n]
            used[0] += n
            v = v.bitcast(dt) if dt != F32 else v
            return v.rearrange(f"p ({names}) -> p {names}", **dict(zip(names.split(), shape)))

        xin = carve("s t d", 2, IT, D)
        xn = carve("s t d", 2, IT, D)
        rest = carve("s t d", 2, IT, D)
        part = carve("s k t d", 2, PARTS, IT, D, dt=BF16)
        xT = carve("s c m", 2, C, IT * P)
        lg = carve("s g t", 2, IT * G, GT)
        choice3T = carve("g k t", NG, PARTS, GT, dt=BF16)

        choiceT = sb("choiceT", [P, TOK], BF16)
        choice = sb("choice", [PARTS * GT, NG, NX], BF16)
        wc = sb("wc", [P, C, NX])
        bc = sb("bc", [P, 1])
        tie = sb("tie", [P, GT])
        b1 = sb("b1", [P, NQ])
        b2 = sb("b2", [P, C, NX])
        idf = sb("idf", [P, P])
        idb = sb("idb", [P, P], BF16)
        jmask = sb("jmask", [P, J])
        st6 = sb("st6", [P, 2, IT, 6])
        mv = sb("mv", [P, 2, IT, 2])
        eps = sb("eps", [P, 1])
        std = sb("std", [P, 2, IT])
        rstd = sb("rstd", [P, 2, IT])
        mx = sb("mx", [P, 2, IT * G])
        w1 = sb("w1", [P, 2, C, P])
        w2 = sb("w2", [P, 2, D])
        hid = sb("hid", [P, 2, NG])
        quads = sb("quads", [P, 2, C * J * NG + J * NG])
        stack = quads[0:PARTS * GT, :, :].rearrange("p s m -> p (s m)").bitcast(BF16)[
            :, 0:2 * GI * G * D].rearrange("p (s g d) -> p s g d", s=2, d=D)
        quad = quads[:, :, 0:C * J * NG].rearrange("p s (c j n) -> p s c j n", c=C, j=J)
        hbd = quads[:, :, C * J * NG:].rearrange("p s (j n) -> p s j n", j=J)
        grp = quads[:, :, 0:C * J * NG].rearrange("p s (g c x) -> p s g c x", g=G, c=C)
        back = sb("back", [P, 2, G, D])
        chf = sb("chf", [P, 2, P])
        xr = sb("xr", [P, 2, D])
        xo = sb("xo", [P, 2, D])
        PS = ctx.enter_context(nc.psum_tensor(f"PS_{tag}", [P, 8, BANK], F32))

        def two_banks(s):
            return PS[:, 2 * s:2 * s + 2, :]

        s_const, s_idb, s_eps = sem("const"), sem("idb"), sem("eps")
        s_seen = sem("seen")
        s_x, s_stat, s_aggr, s_std, s_rstd, s_xn = (
            sems("x"), sem("stat"), sem("aggr"), sem("std"), sem("rstd"), sem("xn"))
        s_hi, s_rest, s_mid, s_lo, s_parts = sem("hi"), sem("rest"), sem("mid"), sem("lo"), sems("parts")
        s_tp, s_xT, s_lgp, s_lg, s_mx, s_choiceT = (
            sem("tp"), sem("xT"), sem("lgp"), sem("lg"), sem("mx"), sem("choiceT"))
        s_choice3T, s_turn, s_choice = sem("choice3T"), sem("turn"), sems("choice")
        s_stack, s_gat, s_gat_c = sems("stack"), sem("gat"), [sem("gat_c0"), sem("gat_c1")]
        s_quad, s_w1, s_w2, s_h, s_hid, s_hbd, s_y, s_ye = (
            sem("quad"), sems("w1"), sems("w2"), sem("h"), sem("hid"), sem("hbd"), sem("y"), sem("ye"))
        s_grp, s_bp, s_back, s_chf, s_sum, s_xr, s_xo, s_out = (
            sem("grp"), sem("bp"), sem("back"), sem("chf"), sem("sum"), sems("xr"), sem("xo"), sems("out"))

        consts = [(wc, wts["wc"]), (bc, wts["bc"]), (tie, wts["tie"]), (b1, wts["b1"]),
                  (b2, wts["b2"]), (idf, wts["idf"]), (jmask, wts["jmask"])]
        CONST = 16 * len(consts)

        GATHER_PRIME = 2 * GI

        def gathered(t):
            return t + 1 + GATHER_PRIME

        block = ctx.enter_context(nc.Block())

        @block.sync
        def _(sp):
            prime(sp, *s_x, *s_parts, *s_w1, *s_w2, *s_xr, *s_out, by=16)
            prime(sp, *s_stack, by=16 * PARTS)

            def load_x(k, s):
                sp.dma_start(xin[:, s], src_items[2 * k + s]).then_inc(s_x[s], 16)

            def store_parts(k, s):
                sp.wait_ge(s_lo, done(2 * k + s))
                for p in range(PARTS):
                    sp.dma_start(parts_items[p, 2 * k + s], part[:, s, p]).then_inc(s_parts[s], 16)

            load_x(0, 0)
            for a, b in consts:
                sp.dma_start(a[:], b).then_inc(s_const, 16)
            load_x(0, 1)
            with sp.Fori(0, NI // 2 - 1) as k:
                for s in range(2):
                    sp.wait_ge(s_xn, done(2 * k + s))
                    load_x(k + 1, s)
                    store_parts(k, s)
            for s in range(2):
                store_parts(NI // 2 - 1, s)

            for s in range(2):
                sp.wait_ge(s_parts[s], 16 + 16 * PARTS * NI // 2)
            with sp.Fori(0, NT // GI // 2) as k:
                for s in range(2):
                    n = 2 * k + s
                    sp.wait_ge(s_gat, gathered(GI * (n - 1) - 1))
                    for p in range(PARTS):
                        sp.dma_start(stack[p * GT:(p + 1) * GT, s], parts_groups[p, n]
                                     ).then_inc(s_stack[s], 16)

            with sp.Fori(0, NQ // 2) as k:
                for s in range(2):
                    q = 2 * k + s
                    sp.wait_ge(s_h, done(q - 2))
                    sp.dma_start(w1[:, s], wts["w1"][q]).then_inc(s_w1[s], 16)
                    sp.wait_ge(s_y, done(q - 2))
                    sp.dma_start(w2[:, s], wts["w2"][q]).then_inc(s_w2[s], 16)

            def load_xr(k, s):
                sp.dma_start(xr[:, s], src_tiles[2 * k + s]).then_inc(s_xr[s], 16)

            def store_xo(k, s):
                sp.wait_ge(s_xo, done(2 * k + s))
                sp.dma_start(dst_tiles[2 * k + s], xo[:, s]).then_inc(s_out[s], 16)

            load_xr(0, 0)
            load_xr(0, 1)
            with sp.Fori(0, NT // 2 - 1) as k:
                for s in range(2):
                    store_xo(k, s)
                    load_xr(k + 1, s)
            for s in range(2):
                store_xo(NT // 2 - 1, s)
            for s in range(2):
                sp.wait_ge(s_out[s], slot_done(NT // 2 - 1, 16))

        @block.gpsimd
        def _(pool):
            prime(pool, s_rest, s_lo, s_chf)
            pool.memset(eps[:], EPS).then_inc(s_eps, 1)

            def less_high(k, s):
                pool.wait_ge(s_hi, done(2 * k + s))
                pool.wait_ge(s_mid, done(2 * k + s - 2))
                pool.wait_ge(s_lo, done(2 * k + s - 2))
                pool.tensor_tensor(rest[:, s], xn[:, s], part[:, s, 0], ALU.subtract).then_inc(s_rest, 1)

            def low(k, s):
                pool.wait_ge(s_mid, done(2 * k + s))
                pool.wait_ge(s_rest, done(2 * k + s))
                pool.tensor_tensor(part[:, s, 2], rest[:, s], part[:, s, 1], ALU.subtract).then_inc(s_lo, 1)

            pipelined(pool, NI, (less_high, 0), (low, 1))

            pool.wait_ge(s_choiceT, done(NI - 1))
            with pool.Fori(0, NT // 2) as k:
                for s in range(2):
                    t = 2 * k + s
                    pool.wait_ge(s_sum, done(t - 2))
                    pool.tensor_copy(chf[:, s], choiceT[:, bass.ds(t * P, P)]).then_inc(s_chf, 1)

        @block.scalar
        def _(act):
            prime(act, s_std, s_hi, s_mid, s_xT, s_gat_c[0], s_hid, s_ye, s_back)
            prime(act, s_choice[0], by=1)
            act.wait_ge(s_eps, 1)
            act.wait_ge(s_const, CONST)

            def deviations(k, s):
                act.wait_ge(s_aggr, done(2 * k + s))
                act.wait_ge(s_rstd, done(2 * k + s - 2))
                act.activation(std[:, s], mv[:, s, :, 1], ACT.Sqrt, bias=eps[:, 0:1]
                               ).then_inc(s_std, 1)

            def high(k, s):
                act.wait_ge(s_xn, done(2 * k + s))
                act.wait_ge(s_parts[s], 16 + 16 * PARTS * k)
                act.activation(part[:, s, 0], xn[:, s], ACT.Copy).then_inc(s_hi, 1)

            def columns(k, s):
                act.wait_ge(s_tp, done(2 * k + s))
                act.wait_ge(s_lgp, done(2 * k + s - 2))
                act.activation(xT[:, s], two_banks(s), ACT.Copy).then_inc(s_xT, 1)

            def middle(k, s):
                act.wait_ge(s_rest, done(2 * k + s))
                act.activation(part[:, s, 1], rest[:, s], ACT.Copy).then_inc(s_mid, 1)

            pipelined(act, NI, (deviations, 0), (columns, 1), (middle, 1), (high, 0))

            with act.Fori(0, NT // 2) as k:
                act.wait_ge(s_turn, done(2 * k))
                act.activation(choice[:, bass.ds(2 * k * G, G), :],
                               PS[0:PARTS * GT, 6, :].rearrange("p (g x) -> p g x", g=G),
                               ACT.Copy).then_inc(s_choice[0], 1)

            with act.Fori(0, NT // 2) as k:
                for s in range(2):
                    t = 2 * k + s
                    act.wait_ge(s_gat, gathered(t))
                    act.activation(PT[:, 0, :, bass.ds(t * G, G)],
                                   PS[:, 2 * s, :].rearrange("p (g x) -> p x g", g=G),
                                   ACT.Copy).then_inc(s_gat_c[0], 1)

            def hidden(k, s):
                act.wait_ge(s_h, done(2 * k + s))
                act.wait_ge(s_hbd, done(2 * k + s - 2))
                act.activation(hid[:, s], PS[:, 4 + s, 0:NG], ACT.Relu,
                               bias=b1[:, bass.ds(2 * k + s, 1)]).then_inc(s_hid, 1)

            def keep(k, s):
                q = 2 * k + s
                act.wait_ge(s_y, done(q))
                act.activation(PT[:, :, bass.ds(q * J, J), :],
                               two_banks(s).rearrange("p c (j n) -> p c j n", j=J),
                               ACT.Copy).then_inc(s_ye, 1)

            pipelined(act, NQ, (hidden, 0), (keep, 1))

            with act.Fori(0, NT // 2) as k:
                for s in range(2):
                    t = 2 * k + s
                    act.wait_ge(s_bp, done(t))
                    act.wait_ge(s_sum, done(t - 2))
                    act.activation(back[:, s], two_banks(s).rearrange("p b (g d) -> p (b g) d", d=D),
                                   ACT.Copy).then_inc(s_back, 1)

        @block.vector
        def _(dve):
            prime(dve, s_choice3T, s_stat, s_aggr, s_rstd, s_xn, s_lg, s_mx, s_choiceT, s_gat_c[1], s_quad,
                  s_hbd, s_grp, s_xo)
            prime(dve, s_choice[1], by=1)
            dve.wait_ge(s_const, CONST)
            dve.tensor_copy(idb[:], idf[:]).then_inc(s_idb, 1)

            def stats(k, s):
                n = 2 * k + s
                dve.wait_ge(s_x[s], slot_done(k, 16))
                for t in range(IT):
                    ins = dve.bn_stats(st6[:, s, t], xin[:, s, t])
                ins.then_inc(s_stat, 1)
                dve.wait_ge(s_stat, done(n))
                dve.sem_inc(s_seen, 1)
                for t in range(IT):
                    ins = dve.bn_aggr(mv[:, s, t], st6[:, s, t])
                ins.then_inc(s_aggr, 1)

            def norm(k, s):
                n = 2 * k + s
                dve.wait_ge(s_std, done(n))
                dve.reciprocal(rstd[:, s], std[:, s]).then_inc(s_rstd, 1)
                dve.wait_ge(s_rstd, done(n))
                dve.wait_ge(s_tp, done(n - 2))
                dve.wait_ge(s_rest, done(n - 2))
                for t in range(IT):
                    ins = dve.tensor_scalar(xn[:, s, t], xin[:, s, t], mv[:, s, t, 0:1],
                                            rstd[:, s, t:t + 1], ALU.subtract, ALU.mult)
                ins.then_inc(s_xn, 1)

            def choose(k, s):
                n = 2 * k + s
                dve.wait_ge(s_lgp, done(n))
                dve.scalar_tensor_tensor(
                    lg[:, s], PS[:, 4 + s, :].rearrange("p (g t) -> p g t", t=GT), bc[:, 0:1],
                    tie[:, None, :].broadcast_to([P, IT * G, GT]), ALU.add, ALU.add
                ).then_inc(s_lg, 1)
                dve.wait_ge(s_lg, done(n))
                dve.tensor_reduce(mx[:, s], lg[:, s], AX.X, ALU.max).then_inc(s_mx, 1)
                dve.wait_ge(s_mx, done(n))
                dve.tensor_tensor(
                    choiceT[:, bass.ds(n * IT * P, IT * P)].rearrange("p (g t) -> p g t", t=GT),
                    lg[:, s], mx[:, s, :, None].broadcast_to([P, IT * G, GT]), ALU.is_equal
                ).then_inc(s_choiceT, 1)
                dve.wait_ge(s_choiceT, done(n))
                dve.tensor_copy(
                    choice3T[:, bass.ds(n * IT * G, IT * G)],
                    choiceT[:, bass.ds(n * IT * P, IT * P)].rearrange("p (g t) -> p g t", t=GT)[:, :, None, :]
                    .broadcast_to([P, IT * G, PARTS, GT])).then_inc(s_choice3T, 1)

            pipelined(dve, NI, (stats, 0), (choose, 2), (norm, 0))

            with dve.Fori(0, NT // 2) as k:
                dve.wait_ge(s_turn, done(2 * k + 1))
                dve.tensor_copy(choice[:, bass.ds((2 * k + 1) * G, G), :],
                                PS[0:PARTS * GT, 7, :].rearrange("p (g x) -> p g x", g=G)
                                ).then_inc(s_choice[1], 1)

            with dve.Fori(0, NT // 2) as k:
                for s in range(2):
                    t = 2 * k + s
                    dve.wait_ge(s_gat, gathered(t))
                    dve.tensor_copy(PT[:, 1, :, bass.ds(t * G, G)],
                                    PS[:, 2 * s + 1, :].rearrange("p (g x) -> p x g", g=G)
                                    ).then_inc(s_gat_c[1], 1)

            def take(k, s):
                q = 2 * k + s
                dve.wait_ge(s_h, done(q - 2))
                dve.tensor_copy(quad[:, s].rearrange("p c j n -> p c (j n)"),
                                PT[:, :, bass.ds(q * J, J), :].rearrange("p c j n -> p c (j n)")
                                ).then_inc(s_quad, 1)

            def spread_hidden(k, s):
                dve.wait_ge(s_hid, done(2 * k + s))
                dve.wait_ge(s_y, done(2 * k + s - 2))
                dve.tensor_tensor(hbd[:, s], hid[:, s, None, :].broadcast_to([P, J, NG]),
                                  jmask[:, :, None].broadcast_to([P, J, NG]), ALU.mult
                                  ).then_inc(s_hbd, 1)

            for c in range(C):
                dve.wait_ge(s_gat_c[c], done(NT - 1))

            pipelined(dve, NQ, (take, 0), (spread_hidden, 1))

            def group(k, s):
                t = 2 * k + s
                dve.wait_ge(s_bp, done(t - 2))
                for c in range(C):
                    ins = dve.tensor_tensor(
                        grp[:, s, :, c, :].rearrange("p g x -> p x g"), PT[:, c, :, bass.ds(t * G, G)],
                        b2[:, c, :, None].broadcast_to([P, NX, G]), ALU.add)
                ins.then_inc(s_grp, 1)

            def result(k, s):
                dve.wait_ge(s_sum, done(2 * k + s))
                dve.wait_ge(s_xr[s], slot_done(k, 16))
                dve.wait_ge(s_out[s], slot_done(k - 1, 16))
                dve.scalar_tensor_tensor(xo[:, s], PS[:, 6 + s, 0:D], 0.5, xr[:, s],
                                         ALU.mult, ALU.add).then_inc(s_xo, 1)

            dve.wait_ge(s_ye, done(NQ - 1))
            pipelined(dve, NT, (group, 0), (result, 2))

        @block.tensor
        def _(pe):
            prime(pe, s_tp, s_lgp, s_turn, s_h, s_y, s_bp, s_sum)
            pe.wait_ge(s_const, CONST)

            prime(pe, s_gat, by=GATHER_PRIME)

            def transposes(k, s):
                pe.wait_ge(s_xn, done(2 * k + s))
                pe.wait_ge(s_xT, done(2 * k + s - 2))
                for c in range(C):
                    for t in range(IT):
                        ins = pe.transpose(PS[:, 2 * s + c, t * P:(t + 1) * P],
                                           xn[:, s, t, c * P:(c + 1) * P], idf[:])
                ins.then_inc(s_tp, 1)

            def logits(k, s):
                pe.wait_ge(s_xT, done(2 * k + s))
                pe.wait_ge(s_lg, done(2 * k + s - 2))
                for c in range(C):
                    ins = pe.matmul(PS[:, 4 + s, :], wc[:, c], xT[:, s, c], start=c == 0, stop=c == C - 1)
                ins.then_inc(s_lgp, 1)

            pipelined(pe, NI, (transposes, 0), (logits, 1))

            pe.wait_ge(s_choice3T, done(NI - 1))
            pe.wait_ge(s_idb, 1)
            with pe.Fori(0, NT // 2) as k:
                for s in range(2):
                    t = 2 * k + s
                    pe.wait_ge(s_choice[s], slot_done(k - 1))
                    for g in range(G):
                        ins = pe.matmul(
                            PS[0:PARTS * GT, 6 + s, g * NX:(g + 1) * NX],
                            choice3T[:, t * G + g].rearrange("p k t -> p (k t)"),
                            idb[:], start=True, stop=True)
                    ins.then_inc(s_turn, 1)

            for s in range(2):
                pe.wait_ge(s_choice[s], slot_done(NT // 2 - 1))
            with pe.Fori(0, NT // GI // 2) as k:
                for i in range(2 * GI):
                    t, m, s = 2 * GI * k + i, i // GI, i % 2
                    if i % GI == 0:
                        pe.wait_ge(s_stack[m], slot_done(k, 16 * PARTS))
                    for c in range(C):
                        pe.wait_ge(s_gat_c[c], done(t - 2))
                        for g in range(G):
                            ins = pe.matmul(PS[:, 2 * s + c, g * NX:(g + 1) * NX],
                                            stack[:, m, i % GI * G + g, c * P:(c + 1) * P],
                                            choice[:, t * G + g, :], start=True, stop=True)
                    ins.then_inc(s_gat, 1)

            def first_product(k, s):
                pe.wait_ge(s_quad, done(2 * k + s))
                pe.wait_ge(s_w1[s], slot_done(k, 16))
                pe.wait_ge(s_hid, done(2 * k + s - 2))
                for c in range(C):
                    for j in range(J):
                        ins = pe.matmul(PS[j * F:(j + 1) * F, 4 + s, 0:NG],
                                        w1[:, s, c, j * F:(j + 1) * F], quad[:, s, c, j],
                                        start=c == 0, stop=c == C - 1)
                ins.then_inc(s_h, 1)

            def second_product(k, s):
                pe.wait_ge(s_hbd, done(2 * k + s))
                pe.wait_ge(s_w2[s], slot_done(k, 16))
                pe.wait_ge(s_ye, done(2 * k + s - 2))
                for c in range(C):
                    ins = pe.matmul(PS[:, 2 * s + c, :], w2[:, s, c * P:(c + 1) * P],
                                    hbd[:, s].rearrange("p j n -> p (j n)"), start=True, stop=True)
                ins.then_inc(s_y, 1)

            pipelined(pe, NQ, (first_product, 0), (second_product, 1))

            def by_expert(k, s):
                pe.wait_ge(s_grp, done(2 * k + s))
                pe.wait_ge(s_back, done(2 * k + s - 2))
                for g in range(G):
                    for c in range(C):
                        at = (g % 2) * D + c * P
                        ins = pe.transpose(PS[:, 2 * s + g // 2, at:at + P], grp[:, s, g, c], idf[:])
                ins.then_inc(s_bp, 1)

            def to_tokens(k, s):
                pe.wait_ge(s_back, done(2 * k + s))
                pe.wait_ge(s_chf, done(2 * k + s))
                pe.wait_ge(s_xo, done(2 * k + s - 2))
                for g in range(G):
                    ins = pe.matmul(PS[g * GT:(g + 1) * GT, 6 + s, 0:D], chf[:, s, g * GT:(g + 1) * GT],
                                    back[:, s, g], start=True, stop=True)
                ins.then_inc(s_sum, 1)

            pipelined(pe, NT, (by_expert, 0), (to_tokens, 1))


def attention_stage(nc, src, dst, wts):
    by_batch = src.rearrange("(b m i) d -> b m i d", b=BATCH, i=DIL)
    src_tiles = src.rearrange("(b m i) d -> i b m d", b=BATCH, i=DIL)
    dst_tiles = dst.rearrange("(b m i) d -> i b m d", b=BATCH, i=DIL)

    with ExitStack() as ctx:
        def sb(name, shape, dt=F32):
            return ctx.enter_context(nc.sbuf_tensor(f"{name}_at", shape, dt))

        def sem(name):
            return ctx.enter_context(nc.semaphore(f"{name}_at"))

        def sems(name, n=2):
            return [sem(f"{name}{s}_") for s in range(n)]

        xnT = sb("xnT", [P, C, DIL, BATCH, P])
        QT = sb("QT", [P, C, DIL, BATCH, P])
        KT = sb("KT", [P, C, DIL, BATCH, P])
        tiles = "p c i b m -> p c (i b) m"
        xin = sb("xin", [P, 2, DIL, D])
        xn = sb("xn", [P, 2, DIL, D])
        st6 = sb("st6", [P, 2, DIL, 6])
        mv = sb("mv", [P, 2, DIL, 2])
        eps = sb("eps", [P, 1])
        std = sb("std", [P, 2, DIL])
        rstd = sb("rstd", [P, 2, DIL])
        idf = sb("idf", [P, P])
        hmask = sb("hmask", [P, HC])
        wqk = sb("wqk", [P, 2, C, 2 * D])
        wv = sb("wv", [P, DIL, C, D])
        wo = sb("wo", [P, DIL, C, D])
        bqk = sb("bqk", [P, DIL, 2 * C])
        bv = sb("bv", [P, DIL, D])
        bo = sb("bo", [P, DIL, D])
        qbd = sb("qbd", [P, 2, H, P])
        prob = sb("prob", [P, NB, HB, P])
        probT = sb("probT", [P, NB, HB, P])
        low = sb("low", [P, 2, H])
        total = sb("total", [P, 2, H])
        scale = sb("scale", [P, 2, H])
        scale_wide = sb("scale_wide", [P, 2, D])
        scaleT = sb("scaleT", [P, D])
        xs = sb("xs", [P, 2, C, P])
        v = sb("v", [P, 2, H, 2 * HD])
        oT = sb("oT", [P, 2, D])
        xr = sb("xr", [P, 2, D])
        xrb = sb("xrb", [P, 2, D])
        xo = sb("xo", [P, 2, D])
        PS = ctx.enter_context(nc.psum_tensor("PS_at", [P, 8, BANK], F32))
        TURN, OUTB, MISC = NB, NB + 2, NB + 3

        s_const, s_set, s_bo, s_x = sem("const"), sem("set"), sem("bo"), sems("x")
        s_seen, s_ready = sem("seen"), sem("ready")
        s_stat, s_aggr, s_std, s_rstd, s_xn, s_tp, s_xT = (
            sem("stat"), sem("aggr"), sem("std"), sem("rstd"), sem("xn"), sem("tp"), sem("xT"))
        s_wqk, s_qp, s_kp, s_q, s_k = (
            sems("wqk"), sem("qp"), sem("kp"), sem("q"), sem("k"))
        s_qbd, s_s, s_low, s_exp, s_turn, s_pT = (
            sem("qbd"), sem("s"), sem("low"), sem("exp"), sem("turn"), sems("pT"))
        s_xs, s_vp, s_v, s_scale, s_wide, s_wideT, s_scaleT, s_pv, s_oT = (
            sem("xs"), sem("vp"), sem("v"), sem("scale"), sem("wide"), sem("wideT"), sem("scaleT"),
            sem("pv"), sem("oT"))
        s_proj, s_xr, s_xrb, s_xo, s_out = sem("proj"), sems("xr"), sem("xrb"), sem("xo"), sems("out")

        consts = [(idf, wts["idf"]), (hmask, wts["hmask"]), (wv, wts["wv"]), (wo, wts["wo"]),
                  (bqk, wts["bqk"]), (bv, wts["bv"]), (bo, wts["bo"])]
        CONST = 16 * len(consts)

        def bank_done(u):
            return u + 1 + 2 * NB

        block = ctx.enter_context(nc.Block())

        @block.sync
        def _(sp):
            prime(sp, *s_x, *s_wqk, *s_xr, *s_out, by=16)

            def load_x(k, s):
                sp.wait_ge(s_xn, done(2 * k + s - 2))
                sp.dma_start(xin[:, s], by_batch[2 * k + s]).then_inc(s_x[s], 16)

            load_x(0, 0)
            load_x(0, 1)
            for a, b in consts:
                sp.dma_start(a[:], b).then_inc(s_const, 16)
            with sp.Fori(1, BATCH // 2) as k:
                for s in range(2):
                    load_x(k, s)
            for s in range(2):
                sp.dma_start(wqk[:, s], wts["wqk"][s]).then_inc(s_wqk[s], 16)
            for i in range(2, DIL):
                sp.wait_ge(s_kp, done(4 * (i - 2) + 3))
                sp.dma_start(wqk[:, i % 2], wts["wqk"][i]).then_inc(s_wqk[i % 2], 16)

            def load_xr(k, s):
                sp.wait_ge(s_xrb, done(2 * k + s - 2))
                sp.dma_start(xr[:, s], src_tiles[k // 4, (k % 4) * 2 + s]).then_inc(s_xr[s], 16)

            def store_xo(k, s):
                sp.wait_ge(s_xo, done(2 * k + s))
                sp.dma_start(dst_tiles[k // 4, (k % 4) * 2 + s], xo[:, s]).then_inc(s_out[s], 16)

            pipelined(sp, NT, (load_xr, 0), (store_xo, 4))
            for s in range(2):
                sp.wait_ge(s_out[s], slot_done(NT // 2 - 1, 16))

        @block.gpsimd
        def _(pool):
            prime(pool, s_qbd, s_xrb)
            pool.memset(eps[:], EPS).then_inc(s_set, 1)
            pool.memset(v[:], 0.0).then_inc(s_set, 1)
            pool.wait_ge(s_const, CONST)
            pool.tensor_scalar(bo[:], bo[:], BRANCH_WEIGHT, None, ALU.mult).then_inc(s_bo, 1)
            pool.wait_ge(s_bo, 1)
            pool.wait_ge(s_q, done(4 * DIL - 1))
            q_tiles = QT[:].rearrange(tiles)

            def one_head_rows(k, s):
                t = 2 * k + s
                pool.wait_ge(s_s, bank_done(NB * (t - 1) - 1))
                pool.sem_inc(s_ready, 1)
                for c in range(C):
                    ins = pool.tensor_tensor(
                        qbd[:, s, c * HC:(c + 1) * HC], q_tiles[:, c, t, None, :].broadcast_to([P, HC, P]),
                        hmask[:, :, None].broadcast_to([P, HC, P]), ALU.mult)
                ins.then_inc(s_qbd, 1)

            def residual(k, s):
                pool.wait_ge(s_xr[s], slot_done(k, 16))
                pool.wait_ge(s_xo, done(2 * k + s - 2))
                pool.sem_inc(s_ready, 1)
                pool.tensor_tensor(xrb[:, s], xr[:, s], bo[:, k // 4], ALU.add).then_inc(s_xrb, 1)

            pipelined(pool, NT, (one_head_rows, 0), (residual, 2))

        @block.scalar
        def _(act):
            prime(act, s_std, s_xT, s_k, s_xs)
            prime(act, s_exp, by=2 * NB)
            prime(act, s_pT[1], by=1)
            act.wait_ge(s_set, 2)

            def deviations(k, s):
                act.wait_ge(s_aggr, done(2 * k + s))
                act.wait_ge(s_rstd, done(2 * k + s - 2))
                act.activation(std[:, s], mv[:, s, :, 1], ACT.Sqrt, bias=eps[:, 0:1]
                               ).then_inc(s_std, 1)

            def columns(k, s):
                act.wait_ge(s_tp, done(2 * k + s))
                act.activation(xnT[:, :, :, 2 * k + s, :],
                               PS[:, 2 * s:2 * s + 2, :].rearrange("p c (i m) -> p c i m", i=DIL),
                               ACT.Copy).then_inc(s_xT, 1)

            pipelined(act, BATCH, (deviations, 0), (columns, 2))

            act.wait_ge(s_const, CONST)
            with act.Fori(0, DIL) as i:
                for c in range(C):
                    for h in range(2):
                        act.wait_ge(s_kp, done(4 * i + 2 * c + h))
                        act.activation(KT[:, c, i, h * HALF:(h + 1) * HALF], PS[:, 6 + h, :].rearrange(
                            "p (b m) -> p b m", m=P), ACT.Identity, bias=bqk[:, i, C + c:C + c + 1]
                        ).then_inc(s_k, 1)

            x_tiles = xnT[:].rearrange(tiles)

            def tile_columns(k, s):
                act.wait_ge(s_vp, done(2 * k + s - 2))
                act.activation(xs[:, s], x_tiles[:, :, 2 * k + s, :], ACT.Copy).then_inc(s_xs, 1)

            def exps(j):
                def f(k, s):
                    u = NB * (2 * k + s) + j
                    act.wait_ge(s_low, bank_done(u))
                    act.wait_ge(s_turn, bank_done(u - NB))
                    act.wait_ge(s_scale, done(2 * k + s - 2))
                    for g in range(HB):
                        h = HB * j + g
                        ins = act.activation(prob[:, j, g], PS[:, j, g * P:(g + 1) * P], ACT.Exp,
                                             bias=low[:, s, h:h + 1], scale=-1.0,
                                             accum_out=total[:, s, h:h + 1])
                    ins.then_inc(s_exp, 1)
                return f

            def turned(j):
                def f(k, s):
                    act.wait_ge(s_turn, bank_done(NB * (2 * k + s) + j))
                    act.activation(probT[:, j].rearrange("p g q -> p (g q)"), PS[:, TURN + 1, :],
                                   ACT.Copy).then_inc(s_pT[1], 1)
                return f

            pipelined(act, NT, (tile_columns, 0), (exps(0), 0), (turned(1), 1), (exps(1), 0),
                      (exps(2), 0), (turned(3), 1), (exps(3), 0))

        @block.vector
        def _(dve):
            prime(dve, s_stat, s_aggr, s_rstd, s_xn, s_q, s_v, s_scale, s_wide, s_scaleT, s_oT, s_xo)
            prime(dve, s_low, by=2 * NB)
            prime(dve, s_pT[0], by=1)

            def stats(k, s):
                n = 2 * k + s
                dve.wait_ge(s_x[s], slot_done(k, 16))
                for t in range(DIL):
                    ins = dve.bn_stats(st6[:, s, t], xin[:, s, t])
                ins.then_inc(s_stat, 1)
                dve.wait_ge(s_stat, done(n))
                dve.sem_inc(s_seen, 1)
                for t in range(DIL):
                    ins = dve.bn_aggr(mv[:, s, t], st6[:, s, t])
                ins.then_inc(s_aggr, 1)

            def norm(k, s):
                n = 2 * k + s
                dve.wait_ge(s_std, done(n))
                dve.reciprocal(rstd[:, s], std[:, s]).then_inc(s_rstd, 1)
                dve.wait_ge(s_rstd, done(n))
                dve.wait_ge(s_tp, done(n - 2))
                for t in range(DIL):
                    ins = dve.tensor_scalar(xn[:, s, t], xin[:, s, t], mv[:, s, t, 0:1],
                                            rstd[:, s, t:t + 1], ALU.subtract, ALU.mult)
                ins.then_inc(s_xn, 1)

            pipelined(dve, BATCH, (stats, 0), (norm, 1))

            dve.wait_ge(s_const, CONST)
            with dve.Fori(0, DIL) as i:
                for c in range(C):
                    for h in range(2):
                        dve.wait_ge(s_qp, done(4 * i + 2 * c + h))
                        dve.tensor_scalar(
                            QT[:, c, i, h * HALF:(h + 1) * HALF].rearrange("p b m -> p (b m)"),
                            PS[:, 4 + h, :], bqk[:, i, c:c + 1], -float(HD) ** -0.5, ALU.add, ALU.mult
                        ).then_inc(s_q, 1)

            def lows(j):
                def f(k, s):
                    u = NB * (2 * k + s) + j
                    dve.wait_ge(s_s, bank_done(u))
                    dve.wait_ge(s_exp, bank_done(u - 2 * NB))
                    dve.tensor_reduce(low[:, s, HB * j:HB * (j + 1)],
                                      PS[:, j, :].rearrange("p (g k) -> p g k", g=HB), AX.X, ALU.min
                                      ).then_inc(s_low, 1)
                return f

            def turned(j):
                def f(k, s):
                    dve.wait_ge(s_turn, bank_done(NB * (2 * k + s) + j))
                    dve.tensor_copy(probT[:, j].rearrange("p g q -> p (g q)"), PS[:, TURN, :]
                                    ).then_inc(s_pT[0], 1)
                return f

            def scales(k, s):
                n = 2 * k + s
                dve.wait_ge(s_exp, bank_done(NB * n + NB - 1))
                dve.wait_ge(s_wide, done(n - 2))
                dve.reciprocal(scale[:, s], total[:, s]).then_inc(s_scale, 1)
                dve.wait_ge(s_scale, done(n))
                dve.wait_ge(s_wideT, done(n - 2))
                dve.tensor_copy(scale_wide[:, s].rearrange("p (h d) -> p h d", h=H),
                                scale[:, s, :, None].broadcast_to([P, H, HD])).then_inc(s_wide, 1)

            def values(k, s):
                dve.wait_ge(s_vp, done(2 * k + s))
                dve.wait_ge(s_pv, done(2 * k + s - 2))
                for o in range(2):
                    odd = "p (h o d) -> p h o d"
                    ins = dve.tensor_tensor(
                        v[:, s].rearrange("p (h o) d -> p h o d", o=2)[:, :, o, o * HD:(o + 1) * HD],
                        PS[:, MISC, 0:D].rearrange(odd, o=2, d=HD)[:, :, o],
                        bv[:, k // 4].rearrange(odd, o=2, d=HD)[:, :, o], ALU.add)
                ins.then_inc(s_v, 1)

            def scaled(k, s):
                n = 2 * k + s
                dve.wait_ge(s_wideT, done(n))
                dve.wait_ge(s_oT, done(n - 1))
                dve.tensor_copy(scaleT[:], PS[:, OUTB, D:2 * D]).then_inc(s_scaleT, 1)
                dve.wait_ge(s_scaleT, done(n))
                dve.wait_ge(s_proj, done(n - 2))
                dve.tensor_tensor(oT[:, s], PS[:, OUTB, 0:D], scaleT[:], ALU.mult).then_inc(s_oT, 1)

            def result(k, s):
                dve.wait_ge(s_proj, done(2 * k + s))
                dve.wait_ge(s_xrb, done(2 * k + s))
                dve.wait_ge(s_out[s], slot_done(k - 1, 16))
                dve.scalar_tensor_tensor(xo[:, s], PS[:, MISC, D:2 * D], BRANCH_WEIGHT, xrb[:, s],
                                         ALU.mult, ALU.add).then_inc(s_xo, 1)

            dve.wait_ge(s_set, 2)
            pipelined(dve, NT, (scaled, 2), (lows(0), 0), (turned(0), 1), (lows(1), 0), (scales, 1),
                      (result, 2), (lows(2), 0), (turned(2), 1), (lows(3), 0), (values, 0))

        @block.tensor
        def _(pe):
            prime(pe, s_tp, s_qp, s_kp, s_vp, s_wideT, s_pv, s_proj)
            prime(pe, s_s, s_turn, by=2 * NB)
            pe.wait_ge(s_const, CONST)

            with pe.Fori(0, BATCH // 2) as k:
                for s in range(2):
                    n = 2 * k + s
                    pe.wait_ge(s_xn, done(n))
                    pe.wait_ge(s_xT, done(n - 2))
                    for c in range(C):
                        for i in range(DIL):
                            ins = pe.transpose(PS[:, 2 * s + c, i * P:(i + 1) * P],
                                               xn[:, s, i, c * P:(c + 1) * P], idf[:])
                    ins.then_inc(s_tp, 1)

            pe.wait_ge(s_xT, done(BATCH - 1))
            with pe.Fori(0, DIL // 2) as k:
                for s in range(2):
                    i = 2 * k + s
                    pe.wait_ge(s_wqk[s], slot_done(k, 16))
                    for c in range(C):
                        for h in range(2):
                            for base, made, read, bank in ((0, s_qp, s_q, 4), (D, s_kp, s_k, 6)):
                                pe.wait_ge(read, done(4 * i + 2 * c + h - 2))
                                at = base + c * P
                                for e in range(C):
                                    ins = pe.matmul(
                                        PS[:, bank + h, :], wqk[:, s, e, at:at + P],
                                        xnT[:, e, i, h * HALF:(h + 1) * HALF].rearrange("p b m -> p (b m)"),
                                        start=e == 0, stop=e == C - 1)
                                ins.then_inc(made, 1)
            k_tiles = KT[:].rearrange(tiles)
            pe.wait_ge(s_q, done(4 * DIL - 1))
            pe.wait_ge(s_k, done(4 * DIL - 1))

            def scores(j):
                def f(k, s):
                    t = 2 * k + s
                    pe.wait_ge(s_qbd, done(t))
                    pe.wait_ge(s_exp, bank_done(NB * (t - 1) + j))
                    for g in range(HB):
                        h = HB * j + g
                        ins = pe.matmul(PS[:, j, g * P:(g + 1) * P], qbd[:, s, h], k_tiles[:, h // HC, t],
                                        start=True, stop=True)
                    ins.then_inc(s_s, 1)
                return f

            def turns(j):
                def f(k, s):
                    t = 2 * k + s
                    pe.wait_ge(s_exp, bank_done(NB * t + j))
                    pe.wait_ge(s_pT[j % 2], slot_done(2 * t + j // 2 - 1))
                    for g in range(HB):
                        ins = pe.transpose(PS[:, TURN + j % 2, g * P:(g + 1) * P], prob[:, j, g], idf[:])
                    ins.then_inc(s_turn, 1)
                return f

            def values(k, s):
                pe.wait_ge(s_xs, done(2 * k + s))
                pe.wait_ge(s_xo, done(2 * k + s - 2))
                for e in range(C):
                    ins = pe.matmul(PS[:, MISC, 0:D], xs[:, s, e], wv[:, k // 4, e], start=e == 0,
                                    stop=e == C - 1)
                ins.then_inc(s_vp, 1)

            def weighted(k, s):
                t = 2 * k + s
                pe.wait_ge(s_v, done(t))
                for o in range(2):
                    pe.wait_ge(s_pT[o], slot_done(2 * t + 1))
                pe.wait_ge(s_oT, done(t - 1))
                for c in range(C):
                    for o in range(2):
                        for r in range(HC // 2):
                            h = c * HC + 2 * r + o
                            ins = pe.matmul(PS[r * 2 * HD:(r + 1) * 2 * HD, OUTB, c * P:(c + 1) * P],
                                            v[:, s, h], probT[:, h // HB, h % HB], start=o == 0, stop=o == 1)
                ins.then_inc(s_pv, 1)

            def scale_rows(k, s):
                pe.wait_ge(s_wide, done(2 * k + s))
                for c in range(C):
                    ins = pe.transpose(PS[:, OUTB, D + c * P:D + (c + 1) * P],
                                       scale_wide[:, s, c * P:(c + 1) * P], idf[:])
                ins.then_inc(s_wideT, 1)

            def project(k, s):
                pe.wait_ge(s_oT, done(2 * k + s))
                t = 2 * k + s
                pe.wait_ge(s_v, done(min(t + 1, NT - 1) if isinstance(k, int) else t + 1))
                for c in range(C):
                    ins = pe.matmul(PS[:, MISC, D:2 * D], oT[:, s, c * P:(c + 1) * P], wo[:, k // 4, c],
                                    start=c == 0, stop=c == C - 1)
                ins.then_inc(s_proj, 1)

            pipelined(pe, NT, (scores(0), 0), (turns(0), 1), (scores(1), 0), (turns(1), 1), (project, 2),
                      (scores(2), 0), (turns(2), 1), (scores(3), 0), (turns(3), 1), (values, 0),
                      (weighted, 1), (scale_rows, 1))


def macaron(nc, x, out, wts):
    x1 = nc.dram_tensor("x1", (TOK, D), F32).ap()
    x2 = nc.dram_tensor("x2", (TOK, D), F32).ap()
    ffn_stage(nc, "a", x, x1, wts)
    attention_stage(nc, x1, x2, wts)
    ffn_stage(nc, "b", x2, out, wts)


_INS = ["x", "wc", "bc", "tie", "w1", "b1", "w2", "b2", "idf", "jmask", "hmask", "wqk", "bqk", "wv", "bv",
        "wo", "bo"]


def kernel(L0_attn_x, L0_attn_Wqkv, L0_attn_bqkv, L0_attn_Wo, L0_attn_bo,
           L0_ffn_Wc, L0_ffn_bc, L0_ffn_W1, L0_ffn_b1, L0_ffn_W2, L0_ffn_b2):
    import concourse.bacc as bacc
    from concourse.bass_utils import run_bass_kernel_spmd

    a = {k: np.asarray(v) for k, v in locals().items() if k.startswith("L0_")}
    f32 = np.float32
    wqkv = a["L0_attn_Wqkv"].reshape(DIL, 3 * D, C, P).transpose(0, 3, 2, 1)
    bqkv = a["L0_attn_bqkv"]
    arrays = {
        "x": a["L0_attn_x"].reshape(TOK, D),
        "wc": a["L0_ffn_Wc"].reshape(C, P, NX).transpose(1, 0, 2),
        "bc": a["L0_ffn_bc"].reshape(NX, 1),
        "tie": np.broadcast_to(np.linspace(0.0, 1e-6, GT, dtype=f32), (P, GT)),
        "w1": a["L0_ffn_W1"].reshape(NQ, J, C, P, F).transpose(0, 3, 2, 1, 4).reshape(NQ, P, C, P),
        "b1": a["L0_ffn_b1"].reshape(NQ, P).T,
        "w2": a["L0_ffn_W2"].reshape(NQ, J, D, F).transpose(0, 1, 3, 2).reshape(NQ, P, D),
        "b2": a["L0_ffn_b2"].reshape(NX, C, P).transpose(2, 1, 0),
        "idf": np.eye(P, dtype=f32),
        "jmask": np.kron(np.eye(J, dtype=f32), np.ones((F, 1), f32)),
        "hmask": np.kron(np.eye(HC, dtype=f32), np.ones((HD, 1), f32)),
        "wqk": wqkv[..., :2 * D],
        "bqk": bqkv[:, :2 * D].reshape(DIL, 2 * C, P).transpose(2, 0, 1),
        "wv": wqkv[..., 2 * D:].transpose(1, 0, 2, 3),
        "bv": np.broadcast_to(bqkv[None, :, 2 * D:], (P, DIL, D)),
        "wo": a["L0_attn_Wo"].reshape(DIL, D, C, P).transpose(3, 0, 2, 1),
        "bo": np.broadcast_to(a["L0_attn_bo"][None], (P, DIL, D)),
    }
    arrays = {f"in_{k}": np.ascontiguousarray(v) for k, v in arrays.items()}
    nc = bacc.Bacc("TRN2", target_bir_lowering=False, num_devices=1)
    aps = {k: nc.dram_tensor(f"in_{k}", arrays[f"in_{k}"].shape, F32, kind="ExternalInput").ap()
           for k in _INS}
    out = nc.dram_tensor("out", (TOK, D), F32, kind="ExternalOutput").ap()
    macaron(nc, aps.pop("x"), out, aps)
    r = run_bass_kernel_spmd(nc, [arrays], core_ids=[0])
    return np.asarray(r.results[0]["out"]).reshape(BATCH, TOK // BATCH, D)
```

```python
from contextlib import ExitStack

import numpy as np
import concourse.bass as bass
from concourse import mybir
from concourse.alu_op_type import AluOpType as ALU

ACT = mybir.ActivationFunctionType
AX = mybir.AxisListType
F32 = mybir.dt.float32
BF16 = mybir.dt.bfloat16

P = 128
BANK = 512
D = 256
C = D // P
TOK = 4096
NT = TOK // P
GT = 32
NG = TOK // GT
G = P // GT
NX = 128
F = 32
J = P // F
NQ = NX // J
PARTS = 3
IT = 4
NI = NT // IT
SL = 4
GI = 2
EPS = 1e-5
BATCH = 8
DIL = 4
H = 16
HD = D // H
HC = P // HD
HB = 4
NB = H // HB
BRANCH_WEIGHT = 1.0 / DIL
HALF = 4


def done(n):
    return n + 3


def slot_done(k, unit=1):
    return (k + 2) * unit


def prime(eng, *sems, by=2):
    for s in sems:
        eng.sem_inc(s, by)


def pipelined(eng, n, *stages, turn=2):
    most = max(lag for _, lag in stages)
    ahead = -(-most // turn) * turn

    def step(m, i, static=True):
        for f, lag in stages:
            if static and not 0 <= turn * m + i - lag < n:
                continue
            f(m + (i - lag) // turn, (i - lag) % turn)

    for v in range(ahead):
        step(v // turn, v % turn)
    with eng.Fori(0, (n - ahead) // turn) as k:
        for i in range(turn):
            step(k + ahead // turn, i, static=False)
    for v in range(n, n + most):
        step(v // turn, v % turn)


def ffn_stage(nc, tag, src, dst, wts):
    parts_d = nc.dram_tensor(f"parts_{tag}", (PARTS, TOK, D), BF16).ap()
    src_items = src.rearrange("(n t p) d -> n p t d", p=P, t=IT)
    src_pairs = src.rearrange("(n t p) d -> n p t d", p=P, t=2)
    dst_pairs = dst.rearrange("(n t p) d -> n p t d", p=P, t=2)
    parts_items = parts_d.rearrange("k (n t p) d -> k n p t d", p=P, t=IT)
    parts_groups = parts_d.rearrange("k (n g t) d -> k n t g d", g=GI * G, t=GT)

    with ExitStack() as ctx:
        def sb(name, shape, dt=F32):
            return ctx.enter_context(nc.sbuf_tensor(f"{name}_{tag}", shape, dt))

        def sem(name):
            return ctx.enter_context(nc.semaphore(f"{name}_{tag}"))

        def sems(name, n=2):
            return [sem(f"{name}{s}_") for s in range(n)]

        PT = sb("PT", [P, C, NX, NG])
        flat = PT[:, :, :, :].rearrange("p c x n -> p (c x n)")
        used = [0]

        def carve(names, *shape, dt=F32):
            n = int(np.prod(shape)) * (2 if dt == BF16 else 4) // 4
            v = flat[:, used[0]:used[0] + n]
            used[0] += n
            v = v.bitcast(dt) if dt != F32 else v
            return v.rearrange(f"p ({names}) -> p {names}", **dict(zip(names.split(), shape)))

        xin = carve("s t d", 4, IT, D)
        xn = carve("s t d", 2, IT, D)
        rest = carve("s t d", 2, IT, D)
        part = carve("n k t d", NI, PARTS, IT, D, dt=BF16)
        xT = carve("s c m", 2, C, IT * P)
        lg = carve("s g t", 2, IT * G, GT)
        choice3T = carve("s g k t", 2, IT * G, PARTS, GT, dt=BF16)

        choiceT = sb("choiceT", [P, TOK], BF16)
        choice = sb("choice", [PARTS * GT, NG, NX], BF16)
        wc = sb("wc", [P, C, NX])
        bc = sb("bc", [P, 1])
        tie = sb("tie", [P, GT])
        b1 = sb("b1", [P, NQ])
        b2 = sb("b2", [P, C, NX])
        idf = sb("idf", [P, P])
        idb = sb("idb", [P, P], BF16)
        jmask = sb("jmask", [P, J])
        st6 = sb("st6", [P, 2, IT, 6])
        mv = sb("mv", [P, 2, IT, 2])
        eps = sb("eps", [P, 1])
        std = sb("std", [P, 2, IT])
        rstd = sb("rstd", [P, 2, IT])
        mx = sb("mx", [P, 2, IT * G])
        w1 = sb("w1", [P, 2, C, P])
        w2 = sb("w2", [P, 2, D])
        hid = sb("hid", [P, 2, NG])
        QUAD = (C + 1) * J * NG
        shared = sb("shared", [P, 2 * (QUAD + G * D)])
        stack = shared[0:PARTS * GT, 0:SL * GI * G * D // 2].bitcast(BF16).rearrange(
            "p (s g d) -> p s g d", s=SL, d=D)
        quads = shared[:, 0:2 * QUAD].rearrange("p (s m) -> p s m", s=2)
        quad = quads[:, :, 0:C * J * NG].rearrange("p s (c j n) -> p s c j n", c=C, j=J)
        hbd = quads[:, :, C * J * NG:].rearrange("p s (j n) -> p s j n", j=J)
        grp = quads[:, :, 0:C * J * NG].rearrange("p s (g c x) -> p s g c x", g=G, c=C)
        back = shared[:, 2 * QUAD:].rearrange("p (s g d) -> p s g d", s=2, g=G)
        chf = sb("chf", [P, 2, P])
        xr = sb("xr", [P, 2, 2, D])
        xo = sb("xo", [P, 2, 2, D])
        PS = ctx.enter_context(nc.psum_tensor(f"PS_{tag}", [P, 8, BANK], F32))

        def two_banks(s):
            return PS[:, 2 * s:2 * s + 2, :]

        s_const, s_idb, s_eps = sem("const"), sem("idb"), sem("eps")
        s_seen = sem("seen")
        s_x, s_stat, s_aggr, s_std, s_rstd, s_xn = (
            sems("x"), sem("stat"), sem("aggr"), sem("std"), sem("rstd"), sem("xn"))
        s_hi, s_rest, s_mid, s_lo, s_parts = sem("hi"), sem("rest"), sem("mid"), sem("lo"), sems("parts")
        s_tp, s_xT, s_lgp, s_lg, s_mx, s_choiceT = (
            sem("tp"), sem("xT"), sem("lgp"), sem("lg"), sem("mx"), sem("choiceT"))
        s_choice3T, s_turn, s_choice = sem("choice3T"), sem("turn"), sem("choice")
        s_stack, s_gat, s_gathered = sems("stack", SL), sem("gat"), sems("gathered", SL)
        s_quad, s_w1, s_w2, s_h, s_hid, s_hbd, s_y, s_ye = (
            sem("quad"), sems("w1"), sems("w2"), sem("h"), sem("hid"), sem("hbd"), sem("y"), sem("ye"))
        s_grp, s_bp, s_back, s_chf, s_sum, s_xr, s_xo, s_out = (
            sems("grp"), sem("bp"), sem("back"), sem("chf"), sem("sum"), sems("xr"), sem("xo"), sems("out"))

        consts = [(wc, wts["wc"]), (bc, wts["bc"]), (tie, wts["tie"]), (b1, wts["b1"]),
                  (b2, wts["b2"]), (idf, wts["idf"]), (jmask, wts["jmask"])]
        CONST = 16 * len(consts)
        HALF_ITEM = IT * G // 2

        def gathered(t):
            return t + 1 + SL

        block = ctx.enter_context(nc.Block())

        @block.sync
        def _(sp):
            prime(sp, *s_x, *s_w1, *s_w2, *s_xr, *s_out, by=16)
            prime(sp, *s_parts, *s_stack, by=16 * PARTS)

            def load_x(k, s):
                sp.wait_ge(s_stat, done(2 * k + s - 2))
                sp.dma_start(xin[:, 2 * (k % 2) + s], src_items[2 * k + s]).then_inc(s_x[s], 16)

            def store_parts(k, s):
                sp.wait_ge(s_lo, done(2 * k + s))
                sp.sem_inc(s_seen, 1)
                sp.wait_ge(s_parts[s], slot_done(k - 1, 16 * PARTS))
                for p in range(PARTS):
                    sp.dma_start(parts_items[p, 2 * k + s], part[:, 2 * k + s, p]).then_inc(s_parts[s], 16)

            load_x(0, 0)
            for a, b in consts:
                sp.dma_start(a[:], b).then_inc(s_const, 16)
            load_x(0, 1)
            load_x(1, 0)
            load_x(1, 1)
            with sp.Fori(2, NI // 2) as k:
                for s in range(2):
                    load_x(k, s)
                    store_parts(k - 2, s)
            for s in range(2):
                store_parts(NI // 2 - 2, s)
            def load_stack(n, i):
                for p in range(PARTS):
                    sp.dma_start(stack[p * GT:(p + 1) * GT, i], parts_groups[p, n]).then_inc(s_stack[i], 16)

            for n in range(SL):
                load_stack(n, n)
            for s in range(2):
                store_parts(NI // 2 - 1, s)
            for s in range(2):
                sp.wait_ge(s_parts[s], slot_done(NI // 2 - 1, 16 * PARTS))
            with sp.Fori(1, NT // GI // SL) as k:
                for i in range(SL):
                    sp.wait_ge(s_gat, gathered(GI * (SL * (k - 1) + i + 1) - 1))
                    load_stack(SL * k + i, i)

            def load_w1(k, s):
                sp.wait_ge(s_h, done(2 * k + s - 2))
                sp.dma_start(w1[:, s], wts["w1"][2 * k + s]).then_inc(s_w1[s], 16)

            def load_w2(k, s):
                sp.wait_ge(s_y, done(2 * k + s - 2))
                sp.dma_start(w2[:, s], wts["w2"][2 * k + s]).then_inc(s_w2[s], 16)

            pipelined(sp, NQ, (load_w1, 0), (load_w2, 2))

            def load_xr(k, s):
                sp.dma_start(xr[:, s], src_pairs[2 * k + s]).then_inc(s_xr[s], 16)

            def store_xo(k, s):
                sp.wait_ge(s_xo, done(2 * (2 * k + s) + 1))
                sp.dma_start(dst_pairs[2 * k + s], xo[:, s]).then_inc(s_out[s], 16)

            for s in range(2):
                load_xr(0, s)
            with sp.Fori(0, NT // 4 - 1) as k:
                for s in range(2):
                    store_xo(k, s)
                    load_xr(k + 1, s)
            for s in range(2):
                store_xo(NT // 4 - 1, s)
            for s in range(2):
                sp.wait_ge(s_out[s], slot_done(NT // 4 - 1, 16))

        @block.gpsimd
        def _(pool):
            prime(pool, s_rest, s_lo, s_grp[1])
            pool.memset(eps[:], EPS).then_inc(s_eps, 1)

            def less_high(k, s):
                pool.wait_ge(s_hi, done(2 * k + s))
                pool.wait_ge(s_mid, done(2 * k + s - 2))
                pool.wait_ge(s_lo, done(2 * k + s - 2))
                pool.sem_inc(s_seen, 1)
                pool.tensor_tensor(rest[:, s], xn[:, s], part[:, 2 * k + s, 0], ALU.subtract
                                   ).then_inc(s_rest, 1)

            def low(k, s):
                pool.wait_ge(s_mid, done(2 * k + s))
                pool.wait_ge(s_rest, done(2 * k + s))
                pool.sem_inc(s_seen, 1)
                pool.tensor_tensor(part[:, 2 * k + s, 2], rest[:, s], part[:, 2 * k + s, 1],
                                   ALU.subtract).then_inc(s_lo, 1)

            pipelined(pool, NI, (less_high, 0), (low, 1))

            pool.wait_ge(s_ye, done(NQ - 1))
            with pool.Fori(0, NT // 2) as k:
                for s in range(2):
                    t = 2 * k + s
                    pool.wait_ge(s_bp, done(t - 2))
                    pool.sem_inc(s_seen, 1)
                    pool.tensor_tensor(
                        grp[:, s, :, 1, :].rearrange("p g x -> p x g"), PT[:, 1, :, bass.ds(t * G, G)],
                        b2[:, 1, :, None].broadcast_to([P, NX, G]), ALU.add).then_inc(s_grp[1], 1)

        @block.scalar
        def _(act):
            prime(act, s_std, s_hi, s_mid, s_xT, s_choice, s_hid, s_ye, s_back, s_chf)
            prime(act, *s_gathered[0::2], by=1)
            act.wait_ge(s_eps, 1)
            act.wait_ge(s_const, CONST)

            def deviations(k, s):
                act.wait_ge(s_aggr, done(2 * k + s))
                act.wait_ge(s_rstd, done(2 * k + s - 2))
                act.activation(std[:, s], mv[:, s, :, 1], ACT.Sqrt, bias=eps[:, 0:1]
                               ).then_inc(s_std, 1)

            def high(k, s):
                act.wait_ge(s_xn, done(2 * k + s))
                act.activation(part[:, 2 * k + s, 0], xn[:, s], ACT.Copy).then_inc(s_hi, 1)

            def columns(k, s):
                act.wait_ge(s_tp, done(2 * k + s))
                act.wait_ge(s_lgp, done(2 * k + s - 2))
                act.activation(xT[:, s], two_banks(s), ACT.Copy).then_inc(s_xT, 1)

            def middle(k, s):
                act.wait_ge(s_rest, done(2 * k + s))
                act.activation(part[:, 2 * k + s, 1], rest[:, s], ACT.Copy).then_inc(s_mid, 1)

            def spread(h):
                def f(k, s):
                    u = 2 * (2 * k + s) + h
                    act.wait_ge(s_turn, done(u))
                    act.activation(choice[:, bass.ds(u * HALF_ITEM, HALF_ITEM), :],
                                   PS[0:PARTS * GT, 6:8, :].rearrange("p b (g x) -> p (b g) x", g=G),
                                   ACT.Copy).then_inc(s_choice, 1)
                return f

            pipelined(act, NI, (deviations, 0), (high, 1), (columns, 1), (spread(0), 4), (middle, 2),
                      (spread(1), 4))

            with act.Fori(0, NT // SL) as k:
                for i in range(0, SL, 2):
                    act.wait_ge(s_gat, gathered(SL * k + i))
                    act.activation(PT[:, :, :, bass.ds((SL * k + i) * G, G)],
                                   two_banks(i).rearrange("p c (g x) -> p c x g", g=G),
                                   ACT.Copy).then_inc(s_gathered[i], 1)

            def hidden(k, s):
                act.wait_ge(s_h, done(2 * k + s))
                act.wait_ge(s_hbd, done(2 * k + s - 2))
                act.activation(hid[:, s], PS[:, 4 + s, 0:NG], ACT.Relu,
                               bias=b1[:, bass.ds(2 * k + s, 1)]).then_inc(s_hid, 1)

            def keep(k, s):
                q = 2 * k + s
                act.wait_ge(s_y, done(q))
                act.activation(PT[:, :, bass.ds(q * J, J), :],
                               two_banks(s).rearrange("p c (j n) -> p c j n", j=J),
                               ACT.Copy).then_inc(s_ye, 1)

            pipelined(act, NQ, (hidden, 0), (keep, 2))

            act.wait_ge(s_choiceT, done(NI - 1))
            with act.Fori(0, NT // 2) as k:
                for s in range(2):
                    t = 2 * k + s
                    act.wait_ge(s_sum, done(t - 2))
                    act.activation(chf[:, s], choiceT[:, bass.ds(t * P, P)], ACT.Copy).then_inc(s_chf, 1)
                    act.wait_ge(s_bp, done(t))
                    act.activation(back[:, s], two_banks(s).rearrange("p b (g d) -> p (b g) d", d=D),
                                   ACT.Copy).then_inc(s_back, 1)

        @block.vector
        def _(dve):
            prime(dve, s_choice3T, s_stat, s_aggr, s_rstd, s_xn, s_lg, s_mx, s_choiceT, s_quad,
                  s_hbd, s_grp[0], s_xo)
            prime(dve, *s_gathered[1::2], by=1)
            dve.wait_ge(s_const, CONST)
            dve.tensor_copy(idb[:], idf[:]).then_inc(s_idb, 1)

            def stats(k, s):
                n = 2 * k + s
                dve.wait_ge(s_x[s], slot_done(k, 16))
                for t in range(IT):
                    ins = dve.bn_stats(st6[:, s, t], xin[:, 2 * (k % 2) + s, t])
                ins.then_inc(s_stat, 1)
                dve.wait_ge(s_stat, done(n))
                dve.sem_inc(s_seen, 1)
                for t in range(IT):
                    ins = dve.bn_aggr(mv[:, s, t], st6[:, s, t])
                ins.then_inc(s_aggr, 1)

            def norm(k, s):
                n = 2 * k + s
                dve.wait_ge(s_std, done(n))
                dve.reciprocal(rstd[:, s], std[:, s]).then_inc(s_rstd, 1)
                dve.wait_ge(s_rstd, done(n))
                dve.wait_ge(s_tp, done(n - 2))
                dve.wait_ge(s_rest, done(n - 2))
                for t in range(IT):
                    ins = dve.tensor_scalar(xn[:, s, t], xin[:, 2 * (k % 2) + s, t], mv[:, s, t, 0:1],
                                            rstd[:, s, t:t + 1], ALU.subtract, ALU.mult)
                ins.then_inc(s_xn, 1)

            def choose(k, s):
                n = 2 * k + s
                dve.wait_ge(s_lgp, done(n))
                dve.scalar_tensor_tensor(
                    lg[:, s], PS[:, 4 + s, :].rearrange("p (g t) -> p g t", t=GT), bc[:, 0:1],
                    tie[:, None, :].broadcast_to([P, IT * G, GT]), ALU.add, ALU.add
                ).then_inc(s_lg, 1)
                dve.wait_ge(s_lg, done(n))
                dve.tensor_reduce(mx[:, s], lg[:, s], AX.X, ALU.max).then_inc(s_mx, 1)
                dve.wait_ge(s_mx, done(n))
                dve.tensor_tensor(
                    choiceT[:, bass.ds(n * IT * P, IT * P)].rearrange("p (g t) -> p g t", t=GT),
                    lg[:, s], mx[:, s, :, None].broadcast_to([P, IT * G, GT]), ALU.is_equal
                ).then_inc(s_choiceT, 1)
                dve.wait_ge(s_choiceT, done(n))
                dve.wait_ge(s_turn, done(2 * (n - 2) + 1))
                dve.sem_inc(s_seen, 1)
                dve.tensor_copy(
                    choice3T[:, s],
                    choiceT[:, bass.ds(n * IT * P, IT * P)].rearrange("p (g t) -> p g t", t=GT)[:, :, None, :]
                    .broadcast_to([P, IT * G, PARTS, GT])).then_inc(s_choice3T, 1)

            pipelined(dve, NI, (stats, 0), (norm, 1), (choose, 3))

            with dve.Fori(0, NT // SL) as k:
                for i in range(1, SL, 2):
                    dve.wait_ge(s_gat, gathered(SL * k + i))
                    dve.tensor_copy(PT[:, :, :, bass.ds((SL * k + i) * G, G)],
                                    two_banks(i).rearrange("p c (g x) -> p c x g", g=G)
                                    ).then_inc(s_gathered[i], 1)

            def take(k, s):
                q = 2 * k + s
                dve.wait_ge(s_h, done(q - 2))
                dve.tensor_copy(quad[:, s].rearrange("p c j n -> p c (j n)"),
                                PT[:, :, bass.ds(q * J, J), :].rearrange("p c j n -> p c (j n)")
                                ).then_inc(s_quad, 1)

            def spread_hidden(k, s):
                dve.wait_ge(s_hid, done(2 * k + s))
                dve.wait_ge(s_y, done(2 * k + s - 2))
                dve.tensor_tensor(hbd[:, s], hid[:, s, None, :].broadcast_to([P, J, NG]),
                                  jmask[:, :, None].broadcast_to([P, J, NG]), ALU.mult
                                  ).then_inc(s_hbd, 1)

            for i in range(SL):
                dve.wait_ge(s_gathered[i], slot_done(NT // SL - 1))

            pipelined(dve, NQ, (take, 0), (spread_hidden, 1))

            def group(k, i):
                t, s = SL * k + i, i % 2
                dve.wait_ge(s_bp, done(t - 2))
                dve.tensor_tensor(
                    grp[:, s, :, 0, :].rearrange("p g x -> p x g"), PT[:, 0, :, bass.ds(t * G, G)],
                    b2[:, 0, :, None].broadcast_to([P, NX, G]), ALU.add).then_inc(s_grp[0], 1)

            def result(k, i):
                dve.wait_ge(s_sum, done(SL * k + i))
                s, half = divmod(i, 2)
                dve.wait_ge(s_xr[s], slot_done(k, 16))
                dve.wait_ge(s_out[s], slot_done(k - 1, 16))
                dve.scalar_tensor_tensor(xo[:, s, half], PS[:, 6 + half, 0:D], 0.5, xr[:, s, half],
                                         ALU.mult, ALU.add).then_inc(s_xo, 1)

            dve.wait_ge(s_ye, done(NQ - 1))
            pipelined(dve, NT, (group, 0), (result, 2), turn=SL)

        @block.tensor
        def _(pe):
            prime(pe, s_tp, s_lgp, s_turn, s_h, s_y, s_bp, s_sum)
            prime(pe, s_gat, by=SL)
            pe.wait_ge(s_const, CONST)
            pe.wait_ge(s_idb, 1)

            def transposes(k, s):
                pe.wait_ge(s_xn, done(2 * k + s))
                pe.wait_ge(s_xT, done(2 * k + s - 2))
                for c in range(C):
                    for t in range(IT):
                        ins = pe.transpose(PS[:, 2 * s + c, t * P:(t + 1) * P],
                                           xn[:, s, t, c * P:(c + 1) * P], idf[:])
                ins.then_inc(s_tp, 1)

            def logits(k, s):
                pe.wait_ge(s_xT, done(2 * k + s))
                pe.wait_ge(s_lg, done(2 * k + s - 2))
                for c in range(C):
                    ins = pe.matmul(PS[:, 4 + s, :], wc[:, c], xT[:, s, c], start=c == 0, stop=c == C - 1)
                ins.then_inc(s_lgp, 1)

            def turns(h):
                def f(k, s):
                    u = 2 * (2 * k + s) + h
                    pe.wait_ge(s_choice3T, done(2 * k + s))
                    pe.wait_ge(s_choice, done(u - 1))
                    for g in range(HALF_ITEM):
                        ins = pe.matmul(PS[0:PARTS * GT, 6 + g // G, g % G * NX:(g % G + 1) * NX],
                                        choice3T[:, s, h * HALF_ITEM + g].rearrange("p k t -> p (k t)"),
                                        idb[:], start=True, stop=True)
                    ins.then_inc(s_turn, 1)
                return f

            pipelined(pe, NI, (transposes, 0), (turns(0), 3), (logits, 1), (turns(1), 3))

            pe.wait_ge(s_choice, done(2 * NI - 1))
            for s in range(2):
                pe.wait_ge(s_parts[s], slot_done(NI // 2 - 1, 16 * PARTS))
            with pe.Fori(0, NT // (GI * SL)) as k8:
                for i8 in range(GI * SL):
                    t, m, i = GI * SL * k8 + i8, i8 // GI, i8 % SL
                    if i8 % GI == 0:
                        pe.wait_ge(s_stack[m], slot_done(k8, 16 * PARTS))
                    pe.wait_ge(s_gathered[i], slot_done(GI * k8 + i8 // SL - 1))
                    for c in range(C):
                        for g in range(G):
                            ins = pe.matmul(PS[:, 2 * i + c, g * NX:(g + 1) * NX],
                                            stack[:, m, i8 % GI * G + g, c * P:(c + 1) * P],
                                            choice[:, t * G + g, :], start=True, stop=True)
                    ins.then_inc(s_gat, 1)

            def first_product(k, s):
                pe.wait_ge(s_quad, done(2 * k + s))
                pe.wait_ge(s_w1[s], slot_done(k, 16))
                pe.wait_ge(s_hid, done(2 * k + s - 2))
                for c in range(C):
                    for j in range(J):
                        ins = pe.matmul(PS[j * F:(j + 1) * F, 4 + s, 0:NG],
                                        w1[:, s, c, j * F:(j + 1) * F], quad[:, s, c, j],
                                        start=c == 0, stop=c == C - 1)
                ins.then_inc(s_h, 1)

            def second_product(k, s):
                pe.wait_ge(s_hbd, done(2 * k + s))
                pe.wait_ge(s_w2[s], slot_done(k, 16))
                pe.wait_ge(s_ye, done(2 * k + s - 2))
                for c in range(C):
                    ins = pe.matmul(PS[:, 2 * s + c, :], w2[:, s, c * P:(c + 1) * P],
                                    hbd[:, s].rearrange("p j n -> p (j n)"), start=True, stop=True)
                ins.then_inc(s_y, 1)

            pipelined(pe, NQ, (first_product, 0), (second_product, 2))

            def by_expert(k, s):
                for c in range(C):
                    pe.wait_ge(s_grp[c], done(2 * k + s))
                pe.wait_ge(s_back, done(2 * k + s - 2))
                for g in range(G):
                    for c in range(C):
                        at = (g % 2) * D + c * P
                        ins = pe.transpose(PS[:, 2 * s + g // 2, at:at + P], grp[:, s, g, c], idf[:])
                ins.then_inc(s_bp, 1)

            def to_tokens(k, s):
                pe.wait_ge(s_back, done(2 * k + s))
                pe.wait_ge(s_chf, done(2 * k + s))
                pe.wait_ge(s_xo, done(2 * k + s - 2))
                for g in range(G):
                    ins = pe.matmul(PS[g * GT:(g + 1) * GT, 6 + s, 0:D], chf[:, s, g * GT:(g + 1) * GT],
                                    back[:, s, g], start=True, stop=True)
                ins.then_inc(s_sum, 1)

            pipelined(pe, NT, (by_expert, 0), (to_tokens, 1))


def attention_stage(nc, src, dst, wts):
    by_batch = src.rearrange("(b m i) d -> b m i d", b=BATCH, i=DIL)
    src_tiles = src.rearrange("(b m i) d -> i b m d", b=BATCH, i=DIL)
    dst_tiles = dst.rearrange("(b m i) d -> i b m d", b=BATCH, i=DIL)

    with ExitStack() as ctx:
        def sb(name, shape, dt=F32):
            return ctx.enter_context(nc.sbuf_tensor(f"{name}_at", shape, dt))

        def sem(name):
            return ctx.enter_context(nc.semaphore(f"{name}_at"))

        def sems(name, n=2):
            return [sem(f"{name}{s}_") for s in range(n)]

        xnT = sb("xnT", [P, C, DIL, BATCH, P])
        QT = sb("QT", [P, C, DIL, BATCH, P])
        KT = sb("KT", [P, C, DIL, BATCH, P])
        tiles = "p c i b m -> p c (i b) m"
        xin = sb("xin", [P, 4, DIL, D])
        xn = sb("xn", [P, 2, DIL, D])
        st6 = sb("st6", [P, 2, DIL, 6])
        mv = sb("mv", [P, 2, DIL, 2])
        eps = sb("eps", [P, 1])
        std = sb("std", [P, 2, DIL])
        rstd = sb("rstd", [P, 2, DIL])
        idf = sb("idf", [P, P])
        hmask = sb("hmask", [P, HC])
        wqk = sb("wqk", [P, 2, C, 2 * D])
        wv = sb("wv", [P, DIL, C, D])
        wo = sb("wo", [P, DIL, C, D])
        bqk = sb("bqk", [P, DIL, 2 * C])
        bv = sb("bv", [P, DIL, D])
        bo = sb("bo", [P, DIL, D])
        qbd = sb("qbd", [P, 2, H, P])
        prob = sb("prob", [P, NB, HB, P])
        probT = sb("probT", [P, NB, HB, P])
        low = sb("low", [P, 2, H])
        total = sb("total", [P, 2, H])
        scale = sb("scale", [P, 2, H])
        scale_wide = sb("scale_wide", [P, 2, D])
        scaleT = sb("scaleT", [P, D])
        xs = sb("xs", [P, 2, C, P])
        v = sb("v", [P, 2, H, 2 * HD])
        oT = sb("oT", [P, 2, D])
        xr = sb("xr", [P, 2, D])
        xrb = sb("xrb", [P, 2, D])
        xo = sb("xo", [P, 2, D])
        PS = ctx.enter_context(nc.psum_tensor("PS_at", [P, 8, BANK], F32))
        TURN, OUTB, MISC = NB, NB + 2, NB + 3

        s_const, s_set, s_bo, s_x = sem("const"), sem("set"), sem("bo"), sems("x")
        s_seen = sem("seen")
        s_stat, s_aggr, s_std, s_rstd, s_xn, s_tp, s_xT = (
            sem("stat"), sem("aggr"), sem("std"), sem("rstd"), sem("xn"), sem("tp"), sem("xT"))
        s_wqk, s_qp, s_kp, s_q, s_k = (
            sems("wqk"), sem("qp"), sem("kp"), sem("q"), sem("k"))
        s_qbd, s_s, s_low, s_exp, s_turn, s_pT = (
            sem("qbd"), sem("s"), sem("low"), sem("exp"), sem("turn"), sems("pT"))
        s_xs, s_vp, s_v, s_scale, s_wide, s_wideT, s_scaleT, s_pv, s_oT = (
            sem("xs"), sem("vp"), sem("v"), sem("scale"), sem("wide"), sem("wideT"), sem("scaleT"),
            sem("pv"), sem("oT"))
        s_proj, s_xr, s_xrb, s_xo, s_out = sem("proj"), sems("xr"), sem("xrb"), sem("xo"), sems("out")

        consts = [(idf, wts["idf"]), (hmask, wts["hmask"]), (wv, wts["wv"]), (wo, wts["wo"]),
                  (bqk, wts["bqk"]), (bv, wts["bv"]), (bo, wts["bo"])]
        CONST = 16 * len(consts)

        def bank_done(u):
            return u + 1 + 2 * NB

        block = ctx.enter_context(nc.Block())

        @block.sync
        def _(sp):
            prime(sp, *s_x, *s_wqk, *s_xr, *s_out, by=16)

            def load_x(k, s):
                sp.wait_ge(s_stat, done(2 * k + s - 2))
                sp.dma_start(xin[:, 2 * (k % 2) + s], by_batch[2 * k + s]).then_inc(s_x[s], 16)

            load_x(0, 0)
            load_x(0, 1)
            for a, b in consts:
                sp.dma_start(a[:], b).then_inc(s_const, 16)
            with sp.Fori(1, BATCH // 2) as k:
                for s in range(2):
                    load_x(k, s)
            for s in range(2):
                sp.dma_start(wqk[:, s], wts["wqk"][s]).then_inc(s_wqk[s], 16)
            for i in range(2, DIL):
                sp.wait_ge(s_kp, done(4 * (i - 2) + 3))
                sp.dma_start(wqk[:, i % 2], wts["wqk"][i]).then_inc(s_wqk[i % 2], 16)

            def load_xr(k, s):
                sp.wait_ge(s_xrb, done(2 * k + s - 2))
                sp.dma_start(xr[:, s], src_tiles[k // 4, (k % 4) * 2 + s]).then_inc(s_xr[s], 16)

            def store_xo(k, s):
                sp.wait_ge(s_xo, done(2 * k + s))
                sp.dma_start(dst_tiles[k // 4, (k % 4) * 2 + s], xo[:, s]).then_inc(s_out[s], 16)

            pipelined(sp, NT, (load_xr, 0), (store_xo, 4))
            for s in range(2):
                sp.wait_ge(s_out[s], slot_done(NT // 2 - 1, 16))

        @block.gpsimd
        def _(pool):
            prime(pool, s_qbd, s_xrb)
            pool.memset(eps[:], EPS).then_inc(s_set, 1)
            pool.memset(v[:], 0.0).then_inc(s_set, 1)
            pool.wait_ge(s_const, CONST)
            pool.tensor_scalar(bo[:], bo[:], BRANCH_WEIGHT, None, ALU.mult).then_inc(s_bo, 1)
            pool.wait_ge(s_bo, 1)
            pool.wait_ge(s_q, done(4 * DIL - 1))
            q_tiles = QT[:].rearrange(tiles)

            def one_head_rows(k, s):
                t = 2 * k + s
                pool.wait_ge(s_s, bank_done(NB * (t - 1) - 1))
                pool.sem_inc(s_seen, 1)
                for c in range(C):
                    ins = pool.tensor_tensor(
                        qbd[:, s, c * HC:(c + 1) * HC], q_tiles[:, c, t, None, :].broadcast_to([P, HC, P]),
                        hmask[:, :, None].broadcast_to([P, HC, P]), ALU.mult)
                ins.then_inc(s_qbd, 1)

            def residual(k, s):
                pool.wait_ge(s_xr[s], slot_done(k, 16))
                pool.wait_ge(s_xo, done(2 * k + s - 2))
                pool.sem_inc(s_seen, 1)
                pool.tensor_tensor(xrb[:, s], xr[:, s], bo[:, k // 4], ALU.add).then_inc(s_xrb, 1)

            pipelined(pool, NT, (one_head_rows, 0), (residual, 2))

        @block.scalar
        def _(act):
            prime(act, s_std, s_xT, s_k, s_xs)
            prime(act, s_exp, by=2 * NB)
            prime(act, s_pT[1], by=1)
            act.wait_ge(s_set, 2)

            def deviations(k, s):
                act.wait_ge(s_aggr, done(2 * k + s))
                act.wait_ge(s_rstd, done(2 * k + s - 2))
                act.activation(std[:, s], mv[:, s, :, 1], ACT.Sqrt, bias=eps[:, 0:1]
                               ).then_inc(s_std, 1)

            def columns(k, s):
                act.wait_ge(s_tp, done(2 * k + s))
                act.activation(xnT[:, :, :, 2 * k + s, :],
                               PS[:, 2 * s:2 * s + 2, :].rearrange("p c (i m) -> p c i m", i=DIL),
                               ACT.Copy).then_inc(s_xT, 1)

            pipelined(act, BATCH, (deviations, 0), (columns, 2))

            act.wait_ge(s_const, CONST)
            with act.Fori(0, DIL) as i:
                for c in range(C):
                    for h in range(2):
                        act.wait_ge(s_kp, done(4 * i + 2 * c + h))
                        act.activation(KT[:, c, i, h * HALF:(h + 1) * HALF], PS[:, 6 + h, :].rearrange(
                            "p (b m) -> p b m", m=P), ACT.Identity, bias=bqk[:, i, C + c:C + c + 1]
                        ).then_inc(s_k, 1)

            x_tiles = xnT[:].rearrange(tiles)

            def tile_columns(k, s):
                act.wait_ge(s_vp, done(2 * k + s - 2))
                act.activation(xs[:, s], x_tiles[:, :, 2 * k + s, :], ACT.Copy).then_inc(s_xs, 1)

            def exps(j):
                def f(k, s):
                    u = NB * (2 * k + s) + j
                    act.wait_ge(s_low, bank_done(u))
                    act.wait_ge(s_turn, bank_done(u - NB))
                    act.wait_ge(s_scale, done(2 * k + s - 2))
                    for g in range(HB):
                        h = HB * j + g
                        ins = act.activation(prob[:, j, g], PS[:, j, g * P:(g + 1) * P], ACT.Exp,
                                             bias=low[:, s, h:h + 1], scale=-1.0,
                                             accum_out=total[:, s, h:h + 1])
                    ins.then_inc(s_exp, 1)
                return f

            def turned(j):
                def f(k, s):
                    act.wait_ge(s_turn, bank_done(NB * (2 * k + s) + j))
                    act.activation(probT[:, j].rearrange("p g q -> p (g q)"), PS[:, TURN + 1, :],
                                   ACT.Copy).then_inc(s_pT[1], 1)
                return f

            pipelined(act, NT, (tile_columns, 0), (exps(0), 0), (turned(1), 1), (exps(1), 0),
                      (exps(2), 0), (turned(3), 1), (exps(3), 0))

        @block.vector
        def _(dve):
            prime(dve, s_stat, s_aggr, s_rstd, s_xn, s_q, s_v, s_scale, s_wide, s_scaleT, s_oT, s_xo)
            prime(dve, s_low, by=2 * NB)
            prime(dve, s_pT[0], by=1)

            def stats(k, s):
                n = 2 * k + s
                dve.wait_ge(s_x[s], slot_done(k, 16))
                for t in range(DIL):
                    ins = dve.bn_stats(st6[:, s, t], xin[:, 2 * (k % 2) + s, t])
                ins.then_inc(s_stat, 1)
                dve.wait_ge(s_stat, done(n))
                dve.sem_inc(s_seen, 1)
                for t in range(DIL):
                    ins = dve.bn_aggr(mv[:, s, t], st6[:, s, t])
                ins.then_inc(s_aggr, 1)

            def norm(k, s):
                n = 2 * k + s
                dve.wait_ge(s_std, done(n))
                dve.reciprocal(rstd[:, s], std[:, s]).then_inc(s_rstd, 1)
                dve.wait_ge(s_rstd, done(n))
                dve.wait_ge(s_tp, done(n - 2))
                for t in range(DIL):
                    ins = dve.tensor_scalar(xn[:, s, t], xin[:, 2 * (k % 2) + s, t], mv[:, s, t, 0:1],
                                            rstd[:, s, t:t + 1], ALU.subtract, ALU.mult)
                ins.then_inc(s_xn, 1)

            pipelined(dve, BATCH, (stats, 0), (norm, 1))

            dve.wait_ge(s_const, CONST)
            with dve.Fori(0, DIL) as i:
                for c in range(C):
                    for h in range(2):
                        dve.wait_ge(s_qp, done(4 * i + 2 * c + h))
                        dve.tensor_scalar(
                            QT[:, c, i, h * HALF:(h + 1) * HALF].rearrange("p b m -> p (b m)"),
                            PS[:, 4 + h, :], bqk[:, i, c:c + 1], -float(HD) ** -0.5, ALU.add, ALU.mult
                        ).then_inc(s_q, 1)

            def lows(j):
                def f(k, s):
                    u = NB * (2 * k + s) + j
                    dve.wait_ge(s_s, bank_done(u))
                    dve.wait_ge(s_exp, bank_done(u - 2 * NB))
                    dve.tensor_reduce(low[:, s, HB * j:HB * (j + 1)],
                                      PS[:, j, :].rearrange("p (g k) -> p g k", g=HB), AX.X, ALU.min
                                      ).then_inc(s_low, 1)
                return f

            def turned(j):
                def f(k, s):
                    dve.wait_ge(s_turn, bank_done(NB * (2 * k + s) + j))
                    dve.tensor_copy(probT[:, j].rearrange("p g q -> p (g q)"), PS[:, TURN, :]
                                    ).then_inc(s_pT[0], 1)
                return f

            def scales(k, s):
                n = 2 * k + s
                dve.wait_ge(s_exp, bank_done(NB * n + NB - 1))
                dve.wait_ge(s_wide, done(n - 2))
                dve.reciprocal(scale[:, s], total[:, s]).then_inc(s_scale, 1)
                dve.wait_ge(s_scale, done(n))
                dve.wait_ge(s_wideT, done(n - 2))
                dve.tensor_copy(scale_wide[:, s].rearrange("p (h d) -> p h d", h=H),
                                scale[:, s, :, None].broadcast_to([P, H, HD])).then_inc(s_wide, 1)

            def values(k, s):
                dve.wait_ge(s_vp, done(2 * k + s))
                dve.wait_ge(s_pv, done(2 * k + s - 2))
                for o in range(2):
                    odd = "p (h o d) -> p h o d"
                    ins = dve.tensor_tensor(
                        v[:, s].rearrange("p (h o) d -> p h o d", o=2)[:, :, o, o * HD:(o + 1) * HD],
                        PS[:, MISC, 0:D].rearrange(odd, o=2, d=HD)[:, :, o],
                        bv[:, k // 4].rearrange(odd, o=2, d=HD)[:, :, o], ALU.add)
                ins.then_inc(s_v, 1)

            def scaled(k, s):
                n = 2 * k + s
                dve.wait_ge(s_wideT, done(n))
                dve.wait_ge(s_oT, done(n - 1))
                dve.tensor_copy(scaleT[:], PS[:, OUTB, D:2 * D]).then_inc(s_scaleT, 1)
                dve.wait_ge(s_scaleT, done(n))
                dve.wait_ge(s_proj, done(n - 2))
                dve.tensor_tensor(oT[:, s], PS[:, OUTB, 0:D], scaleT[:], ALU.mult).then_inc(s_oT, 1)

            def result(k, s):
                dve.wait_ge(s_proj, done(2 * k + s))
                dve.wait_ge(s_xrb, done(2 * k + s))
                dve.wait_ge(s_out[s], slot_done(k - 1, 16))
                dve.scalar_tensor_tensor(xo[:, s], PS[:, MISC, D:2 * D], BRANCH_WEIGHT, xrb[:, s],
                                         ALU.mult, ALU.add).then_inc(s_xo, 1)

            dve.wait_ge(s_set, 2)
            pipelined(dve, NT, (scaled, 2), (lows(0), 0), (turned(0), 1), (lows(1), 0), (scales, 1),
                      (result, 2), (lows(2), 0), (turned(2), 1), (lows(3), 0), (values, 0))

        @block.tensor
        def _(pe):
            prime(pe, s_tp, s_qp, s_kp, s_vp, s_wideT, s_pv, s_proj)
            prime(pe, s_s, s_turn, by=2 * NB)
            pe.wait_ge(s_const, CONST)

            with pe.Fori(0, BATCH // 2) as k:
                for s in range(2):
                    n = 2 * k + s
                    pe.wait_ge(s_xn, done(n))
                    pe.wait_ge(s_xT, done(n - 2))
                    for c in range(C):
                        for i in range(DIL):
                            ins = pe.transpose(PS[:, 2 * s + c, i * P:(i + 1) * P],
                                               xn[:, s, i, c * P:(c + 1) * P], idf[:])
                    ins.then_inc(s_tp, 1)

            pe.wait_ge(s_xT, done(BATCH - 1))
            with pe.Fori(0, DIL // 2) as k:
                for s in range(2):
                    i = 2 * k + s
                    pe.wait_ge(s_wqk[s], slot_done(k, 16))
                    for c in range(C):
                        for h in range(2):
                            for base, made, read, bank in ((0, s_qp, s_q, 4), (D, s_kp, s_k, 6)):
                                pe.wait_ge(read, done(4 * i + 2 * c + h - 2))
                                at = base + c * P
                                for e in range(C):
                                    ins = pe.matmul(
                                        PS[:, bank + h, :], wqk[:, s, e, at:at + P],
                                        xnT[:, e, i, h * HALF:(h + 1) * HALF].rearrange("p b m -> p (b m)"),
                                        start=e == 0, stop=e == C - 1)
                                ins.then_inc(made, 1)
            k_tiles = KT[:].rearrange(tiles)
            pe.wait_ge(s_q, done(4 * DIL - 1))
            pe.wait_ge(s_k, done(4 * DIL - 1))

            def scores(j):
                def f(k, s):
                    t = 2 * k + s
                    pe.wait_ge(s_qbd, done(t))
                    pe.wait_ge(s_exp, bank_done(NB * (t - 1) + j))
                    for g in range(HB):
                        h = HB * j + g
                        ins = pe.matmul(PS[:, j, g * P:(g + 1) * P], qbd[:, s, h], k_tiles[:, h // HC, t],
                                        start=True, stop=True)
                    ins.then_inc(s_s, 1)
                return f

            def turns(j):
                def f(k, s):
                    t = 2 * k + s
                    pe.wait_ge(s_exp, bank_done(NB * t + j))
                    pe.wait_ge(s_pT[j % 2], slot_done(2 * t + j // 2 - 1))
                    for g in range(HB):
                        ins = pe.transpose(PS[:, TURN + j % 2, g * P:(g + 1) * P], prob[:, j, g], idf[:])
                    ins.then_inc(s_turn, 1)
                return f

            def values(k, s):
                pe.wait_ge(s_xs, done(2 * k + s))
                pe.wait_ge(s_xo, done(2 * k + s - 2))
                for e in range(C):
                    ins = pe.matmul(PS[:, MISC, 0:D], xs[:, s, e], wv[:, k // 4, e], start=e == 0,
                                    stop=e == C - 1)
                ins.then_inc(s_vp, 1)

            def weighted(k, s):
                t = 2 * k + s
                pe.wait_ge(s_v, done(t))
                for o in range(2):
                    pe.wait_ge(s_pT[o], slot_done(2 * t + 1))
                pe.wait_ge(s_oT, done(t - 1))
                for c in range(C):
                    for o in range(2):
                        for r in range(HC // 2):
                            h = c * HC + 2 * r + o
                            ins = pe.matmul(PS[r * 2 * HD:(r + 1) * 2 * HD, OUTB, c * P:(c + 1) * P],
                                            v[:, s, h], probT[:, h // HB, h % HB], start=o == 0, stop=o == 1)
                ins.then_inc(s_pv, 1)

            def scale_rows(k, s):
                pe.wait_ge(s_wide, done(2 * k + s))
                for c in range(C):
                    ins = pe.transpose(PS[:, OUTB, D + c * P:D + (c + 1) * P],
                                       scale_wide[:, s, c * P:(c + 1) * P], idf[:])
                ins.then_inc(s_wideT, 1)

            def project(k, s):
                pe.wait_ge(s_oT, done(2 * k + s))
                t = 2 * k + s
                pe.wait_ge(s_v, done(min(t + 1, NT - 1) if isinstance(k, int) else t + 1))
                for c in range(C):
                    ins = pe.matmul(PS[:, MISC, D:2 * D], oT[:, s, c * P:(c + 1) * P], wo[:, k // 4, c],
                                    start=c == 0, stop=c == C - 1)
                ins.then_inc(s_proj, 1)

            pipelined(pe, NT, (scores(0), 0), (turns(0), 1), (scores(1), 0), (turns(1), 1), (project, 2),
                      (scores(2), 0), (turns(2), 1), (scores(3), 0), (turns(3), 1), (values, 0),
                      (weighted, 1), (scale_rows, 1))


def macaron(nc, x, out, wts):
    x1 = nc.dram_tensor("x1", (TOK, D), F32).ap()
    x2 = nc.dram_tensor("x2", (TOK, D), F32).ap()
    ffn_stage(nc, "a", x, x1, wts)
    attention_stage(nc, x1, x2, wts)
    ffn_stage(nc, "b", x2, out, wts)


_INS = ["x", "wc", "bc", "tie", "w1", "b1", "w2", "b2", "idf", "jmask", "hmask", "wqk", "bqk", "wv", "bv",
        "wo", "bo"]


def kernel(L0_attn_x, L0_attn_Wqkv, L0_attn_bqkv, L0_attn_Wo, L0_attn_bo,
           L0_ffn_Wc, L0_ffn_bc, L0_ffn_W1, L0_ffn_b1, L0_ffn_W2, L0_ffn_b2):
    import concourse.bacc as bacc
    from concourse.bass_utils import run_bass_kernel_spmd

    a = {k: np.asarray(v) for k, v in locals().items() if k.startswith("L0_")}
    f32 = np.float32
    wqkv = a["L0_attn_Wqkv"].reshape(DIL, 3 * D, C, P).transpose(0, 3, 2, 1)
    bqkv = a["L0_attn_bqkv"]
    arrays = {
        "x": a["L0_attn_x"].reshape(TOK, D),
        "wc": a["L0_ffn_Wc"].reshape(C, P, NX).transpose(1, 0, 2),
        "bc": a["L0_ffn_bc"].reshape(NX, 1),
        "tie": np.broadcast_to(np.linspace(0.0, 1e-6, GT, dtype=f32), (P, GT)),
        "w1": a["L0_ffn_W1"].reshape(NQ, J, C, P, F).transpose(0, 3, 2, 1, 4).reshape(NQ, P, C, P),
        "b1": a["L0_ffn_b1"].reshape(NQ, P).T,
        "w2": a["L0_ffn_W2"].reshape(NQ, J, D, F).transpose(0, 1, 3, 2).reshape(NQ, P, D),
        "b2": a["L0_ffn_b2"].reshape(NX, C, P).transpose(2, 1, 0),
        "idf": np.eye(P, dtype=f32),
        "jmask": np.kron(np.eye(J, dtype=f32), np.ones((F, 1), f32)),
        "hmask": np.kron(np.eye(HC, dtype=f32), np.ones((HD, 1), f32)),
        "wqk": wqkv[..., :2 * D],
        "bqk": bqkv[:, :2 * D].reshape(DIL, 2 * C, P).transpose(2, 0, 1),
        "wv": wqkv[..., 2 * D:].transpose(1, 0, 2, 3),
        "bv": np.broadcast_to(bqkv[None, :, 2 * D:], (P, DIL, D)),
        "wo": a["L0_attn_Wo"].reshape(DIL, D, C, P).transpose(3, 0, 2, 1),
        "bo": np.broadcast_to(a["L0_attn_bo"][None], (P, DIL, D)),
    }
    arrays = {f"in_{k}": np.ascontiguousarray(v) for k, v in arrays.items()}
    nc = bacc.Bacc("TRN2", target_bir_lowering=False, num_devices=1)
    aps = {k: nc.dram_tensor(f"in_{k}", arrays[f"in_{k}"].shape, F32, kind="ExternalInput").ap()
           for k in _INS}
    out = nc.dram_tensor("out", (TOK, D), F32, kind="ExternalOutput").ap()
    macaron(nc, aps.pop("x"), out, aps)
    r = run_bass_kernel_spmd(nc, [arrays], core_ids=[0])
    return np.asarray(r.results[0]["out"]).reshape(BATCH, TOK // BATCH, D)
```

```python
from contextlib import ExitStack

import numpy as np
import concourse.bass as bass
from concourse import mybir
from concourse.alu_op_type import AluOpType as ALU

ACT = mybir.ActivationFunctionType
AX = mybir.AxisListType
F32 = mybir.dt.float32
BF16 = mybir.dt.bfloat16
F32R = mybir.dt.float32r

P = 128
BANK = 512
D = 256
C = D // P
TOK = 4096
NT = TOK // P
GT = 32
NG = TOK // GT
G = P // GT
NX = 128
F = 32
J = P // F
NQ = NX // J
PARTS = 3
IT = 4
NI = NT // IT
SL = 4
GI = 2
EPS = 1e-5
BATCH = 8
DIL = 4
H = 16
HD = D // H
HC = P // HD
HB = 4
NB = H // HB
BRANCH_WEIGHT = 1.0 / DIL
HALF = 4
QK = 2
PAIRS = 6


def done(n):
    return n + 3


def slot_done(k, unit=1):
    return (k + 2) * unit


def prime(eng, *sems, by=2):
    for s in sems:
        eng.sem_inc(s, by)


def pipelined(eng, n, *stages, turn=2):
    most = max(lag for _, lag in stages)
    ahead = -(-most // turn) * turn

    def step(m, i, static=True):
        for f, lag in stages:
            if static and not 0 <= turn * m + i - lag < n:
                continue
            f(m + (i - lag) // turn, (i - lag) % turn)

    for v in range(ahead):
        step(v // turn, v % turn)
    with eng.Fori(0, (n - ahead) // turn) as k:
        for i in range(turn):
            step(k + ahead // turn, i, static=False)
    for v in range(n, n + most):
        step(v // turn, v % turn)


def ffn_stage(nc, tag, src, dst, wts, s_seen):
    parts_d = nc.dram_tensor(f"parts_{tag}", (NI, PARTS, GT, G, IT * D), BF16).ap()
    src_items = src.rearrange("(n g j t) d -> n g t j d", g=G, j=IT, t=GT)
    src_pairs = src.rearrange("(n t p) d -> n p t d", p=P, t=2)
    dst_pairs = dst.rearrange("(n t p) d -> n p t d", p=P, t=2)
    parts_items = parts_d.rearrange("n k t g m -> n (t g) k m")
    parts_rows = parts_d.rearrange("n k t g m -> n (k t) (g m)")

    with ExitStack() as ctx:
        def sb(name, shape, dt=F32):
            return ctx.enter_context(nc.sbuf_tensor(f"{name}_{tag}", shape, dt))

        def sem(name):
            return nc.alloc_semaphore(f"{name}_{tag}")

        def sems(name, n=2):
            return [sem(f"{name}{s}_") for s in range(n)]

        PT = sb("PT", [P, C, NX, NG])
        flat = PT[:, :, :, :].rearrange("p c x n -> p (c x n)")
        used = [0]

        def carve(names, *shape, dt=F32):
            n = int(np.prod(shape)) * (2 if dt == BF16 else 4) // 4
            v = flat[:, used[0]:used[0] + n]
            used[0] += n
            v = v.bitcast(dt) if dt != F32 else v
            return v.rearrange(f"p ({names}) -> p {names}", **dict(zip(names.split(), shape)))

        xin = carve("s t d", 4, IT, D)
        xn = carve("s t d", 2, IT, D)
        rest = carve("s t d", 2, IT, D)
        part = carve("n k t d", NI, PARTS, IT, D, dt=BF16)
        xT = carve("s c m", 2, C, IT * P)
        lg = carve("s g t", 2, IT * G, GT)
        choice3T = carve("s g k t", 2, IT * G, PARTS, GT, dt=BF16)

        choiceT = sb("choiceT", [P, TOK], BF16)
        choice_mem = sb("choice", [P, NG, NX], BF16)
        choice = choice_mem[0:PARTS * GT]
        wc = sb("wc", [P, C, NX])
        bc = sb("bc", [P, 1])
        tie = sb("tie", [P, GT])
        b1 = sb("b1", [P, NQ])
        b2 = sb("b2", [P, C, NX])
        idf = sb("idf", [P, P])
        idb = sb("idb", [P, P], BF16)
        jmask = sb("jmask", [P, J])
        st6 = sb("st6", [P, 2, IT, 6])
        mv = sb("mv", [P, 2, IT, 2])
        eps = sb("eps", [P, 1])
        std = sb("std", [P, 2, IT])
        rstd = sb("rstd", [P, 2, IT])
        mx = sb("mx", [P, 2, IT * G])
        w1 = sb("w1", [P, 2, C, P])
        w2 = sb("w2", [P, 2, D])
        stack = sb("stack", [PARTS * GT, SL, GI * G, D], BF16)
        hbd, hbd_lo = sb("hbd", [P, 2, J, NG], F32R), sb("hbd_lo", [P, 2, J, NG], F32R)
        w2_hi, w2_lo = sb("w2_hi", [P, 4, D], F32R), sb("w2_lo", [P, 4, D], F32R)
        choice_f32 = choice_mem[:].rearrange("p g x -> p (g x)").bitcast(F32)
        used[0] = 0

        def late(names, *shape):
            n = int(np.prod(shape))
            v = choice_f32[:, used[0]:used[0] + n]
            used[0] += n
            return v.rearrange(f"p ({names}) -> p {names}", **dict(zip(names.split(), shape)))

        quad = late("s c j n", 2, C, J, NG)
        hid = late("s n", 4, NG)
        hid_hi = late("s n", 4, NG)
        grp = late("s g c x", 2, G, C, NX)
        back = late("s g d", 2, G, D)
        xr = late("s t d", 2, 2, D)
        xo = quad.rearrange("p s c j n -> p (s c j n)")[:, 0:4 * D].rearrange(
            "p (s t d) -> p s t d", s=2, t=2)
        chf = hid[:, 0:2]
        PS = ctx.enter_context(nc.psum_tensor(f"PS_{tag}", [P, 8, BANK], F32))

        def two_banks(s):
            return PS[:, 2 * s:2 * s + 2, :]

        s_const, s_set = sem("const"), sem("set")
        s_x, s_stat, s_aggr, s_std, s_rstd, s_xn = (
            sems("x"), sem("stat"), sem("aggr"), sem("std"), sem("rstd"), sem("xn"))
        s_hi, s_rest, s_mid, s_lo, s_parts = sem("hi"), sem("rest"), sem("mid"), sem("lo"), sems("parts")
        s_tp, s_xT, s_lgp, s_lg, s_mx, s_choiceT = (
            sem("tp"), sem("xT"), sem("lgp"), sem("lg"), sem("mx"), sem("choiceT"))
        s_choice3T, s_turn, s_choice = sem("choice3T"), sem("turn"), sem("choice")
        s_stack, s_gat, s_gathered = sems("stack", SL), sem("gat"), sems("gathered", SL)
        s_quad, s_w1, s_w2, s_h, s_hid, s_hbd, s_y, s_ye = (
            sem("quad"), sems("w1"), sems("w2"), sem("h"), sem("hid"), sem("hbd"), sem("y"), sem("ye"))
        s_hid_lo, s_hbd_lo, s_w2_hi, s_w2_lo = sem("hid_lo"), sem("hbd_lo"), sem("w2_hi"), sem("w2_lo")
        s_grp, s_bp, s_back, s_chf, s_sum, s_xr, s_xo, s_out = (
            sems("grp"), sem("bp"), sem("back"), sem("chf"), sem("sum"), sems("xr"), sem("xo"), sems("out"))

        consts = [(idf, wts["idf"]), (wc, wts["wc"]), (bc, wts["bc"]), (tie, wts["tie"])]
        late_consts = [(b1, wts["b1"]), (b2, wts["b2"]), (jmask, wts["jmask"])]
        CONST = 16 * len(consts)
        ALL_CONST = CONST + 16 * len(late_consts)

        def quad_done(q):
            return q + 1 + 4

        def choice_turned(t):
            return t + 1 + 2 * IT

        def gathered(t):
            return t + 1 + SL

        block = ctx.enter_context(nc.Block())

        @block.sync
        def _(sp):
            prime(sp, *s_w1, *s_w2, *s_xr, *s_out, *s_parts, *s_stack, by=16)
            prime(sp, *s_x, by=16 * G)

            def load_x(k, s):
                sp.wait_ge(s_stat, done(2 * k + s - 2))
                for g in range(G):
                    sp.dma_start(xin[g::G, 2 * (k % 2) + s], src_items[2 * k + s, g]).then_inc(s_x[s], 16)

            def store_parts(k, s):
                sp.wait_ge(s_lo, done(2 * k + s))
                sp.sem_inc(s_seen, 1)
                sp.wait_ge(s_parts[s], slot_done(k - 1, 16))
                sp.dma_start(parts_items[2 * k + s], part[:, 2 * k + s].rearrange("p k t d -> p k (t d)")
                             ).then_inc(s_parts[s], 16)

            load_x(0, 0)
            load_x(0, 1)
            for a, b in consts:
                sp.dma_start(a[:], b).then_inc(s_const, 16)
            load_x(1, 0)
            load_x(1, 1)
            sp.wait_ge(s_const, CONST)
            for a, b in late_consts:
                sp.dma_start(a[:], b).then_inc(s_const, 16)
            with sp.Fori(2, NI // 2) as k:
                for s in range(2):
                    load_x(k, s)
                    store_parts(k - 2, s)
            for s in range(2):
                store_parts(NI // 2 - 2, s)
            def load_stack(k, i):
                n, part_of = 2 * k + i // 2, i % 2 * GI * G * D
                sp.dma_start(stack[:, i].rearrange("p g d -> p (g d)"),
                             parts_rows[n, :, part_of:part_of + GI * G * D]).then_inc(s_stack[i], 16)

            for s in range(2):
                store_parts(NI // 2 - 1, s)
            for i in range(SL):
                load_stack(0, i)
            for s in range(2):
                sp.wait_ge(s_parts[s], slot_done(NI // 2 - 1, 16))
            with sp.Fori(1, NT // GI // SL) as k:
                for i in range(SL):
                    sp.wait_ge(s_gat, gathered(GI * (SL * (k - 1) + i + 1) - 1))
                    load_stack(k, i)

            def load_w1(k, s):
                sp.wait_ge(s_h, quad_done(2 * k + s - 2))
                sp.dma_start(w1[:, s], wts["w1"][2 * k + s]).then_inc(s_w1[s], 16)

            def load_w2(k, s):
                sp.wait_ge(s_w2_lo, quad_done(2 * k + s - 2))
                sp.dma_start(w2[:, s], wts["w2"][2 * k + s]).then_inc(s_w2[s], 16)

            pipelined(sp, NQ, (load_w1, 0), (load_w2, 0))

            def load_xr(k, s):
                sp.dma_start(xr[:, s], src_pairs[2 * k + s]).then_inc(s_xr[s], 16)

            def store_xo(k, s):
                sp.wait_ge(s_xo, done(2 * (2 * k + s) + 1))
                sp.dma_start(dst_pairs[2 * k + s], xo[:, s]).then_inc(s_out[s], 16)

            for s in range(2):
                load_xr(0, s)
            with sp.Fori(0, NT // 4 - 1) as k:
                for s in range(2):
                    store_xo(k, s)
                    load_xr(k + 1, s)
            for s in range(2):
                store_xo(NT // 4 - 1, s)
            for s in range(2):
                sp.wait_ge(s_out[s], slot_done(NT // 4 - 1, 16))

        @block.gpsimd
        def _(pool):
            prime(pool, s_rest, s_lo, s_grp[1])
            prime(pool, s_hbd_lo, by=4)
            pool.memset(eps[:], EPS).then_inc(s_set, 1)
            pool.wait_ge(s_const, CONST)
            pool.tensor_copy(idb[:], idf[:]).then_inc(s_set, 1)

            def less_high(k, s):
                pool.wait_ge(s_hi, done(2 * k + s))
                pool.wait_ge(s_mid, done(2 * k + s - 2))
                pool.wait_ge(s_lo, done(2 * k + s - 2))
                pool.sem_inc(s_seen, 1)
                pool.tensor_tensor(rest[:, s], xn[:, s], part[:, 2 * k + s, 0], ALU.subtract
                                   ).then_inc(s_rest, 1)

            def low(k, s):
                pool.wait_ge(s_mid, done(2 * k + s))
                pool.wait_ge(s_rest, done(2 * k + s))
                pool.sem_inc(s_seen, 1)
                pool.tensor_tensor(part[:, 2 * k + s, 2], rest[:, s], part[:, 2 * k + s, 1],
                                   ALU.subtract).then_inc(s_lo, 1)

            pipelined(pool, NI, (less_high, 0), (low, 1))

            pool.wait_ge(s_const, ALL_CONST)

            def spread_low(k, i):
                pool.wait_ge(s_hid_lo, quad_done(4 * k + i))
                pool.wait_ge(s_y, quad_done(4 * k + i - 2))
                pool.sem_inc(s_seen, 1)
                pool.tensor_tensor(hbd_lo[:, i % 2], hid[:, i, None, :].broadcast_to([P, J, NG]),
                                   jmask[:, :, None].broadcast_to([P, J, NG]), ALU.mult
                                   ).then_inc(s_hbd_lo, 1)

            pipelined(pool, NQ, (spread_low, 0), turn=4)

            pool.wait_ge(s_ye, quad_done(NQ - 1))
            with pool.Fori(0, NT // 2) as k:
                for s in range(2):
                    t = 2 * k + s
                    pool.wait_ge(s_bp, done(t - 2))
                    pool.sem_inc(s_seen, 1)
                    pool.tensor_tensor(
                        grp[:, s, :, 1, :].rearrange("p g x -> p x g"), PT[:, 1, :, bass.ds(t * G, G)],
                        b2[:, 1, :, None].broadcast_to([P, NX, G]), ALU.add).then_inc(s_grp[1], 1)

        @block.scalar
        def _(act):
            prime(act, s_std, s_hi, s_mid, s_xT, s_choice, s_back, s_chf)
            prime(act, s_hid, s_w2_hi, s_ye, by=4)
            prime(act, *s_gathered[0::2], by=1)
            act.wait_ge(s_set, 1)

            def deviations(k, s):
                act.wait_ge(s_aggr, done(2 * k + s))
                act.wait_ge(s_rstd, done(2 * k + s - 2))
                act.activation(std[:, s], mv[:, s, :, 1], ACT.Sqrt, bias=eps[:, 0:1]
                               ).then_inc(s_std, 1)

            def high(k, s):
                act.wait_ge(s_xn, done(2 * k + s))
                act.activation(part[:, 2 * k + s, 0], xn[:, s], ACT.Copy).then_inc(s_hi, 1)

            def columns(k, s):
                act.wait_ge(s_tp, done(2 * k + s))
                act.wait_ge(s_lgp, done(2 * k + s - 2))
                act.activation(xT[:, s], two_banks(s), ACT.Copy).then_inc(s_xT, 1)

            def middle(k, s):
                act.wait_ge(s_rest, done(2 * k + s))
                act.activation(part[:, 2 * k + s, 1], rest[:, s], ACT.Copy).then_inc(s_mid, 1)

            def spread(h):
                def f(k, s):
                    t = IT * (2 * k + s) + h
                    act.wait_ge(s_turn, choice_turned(t))
                    act.activation(choice[:, bass.ds(t * G, G), :],
                                   PS[0:PARTS * GT, 6 + h % 2, :].rearrange("p (g x) -> p g x", g=G),
                                   ACT.Copy).then_inc(s_choice, 1)
                return f

            pipelined(act, NI, (high, 1), (columns, 1), (spread(0), 4), (spread(1), 4), (deviations, 0),
                      (middle, 2), (spread(2), 4), (spread(3), 4))

            with act.Fori(0, NT // SL) as k:
                for i in range(0, SL, 2):
                    act.wait_ge(s_gat, gathered(SL * k + i))
                    act.activation(PT[:, :, :, bass.ds((SL * k + i) * G, G)],
                                   two_banks(i).rearrange("p c (g x) -> p c x g", g=G),
                                   ACT.Copy).then_inc(s_gathered[i], 1)

            act.wait_ge(s_const, ALL_CONST)

            def hidden(k, i):
                q = 4 * k + i
                act.wait_ge(s_h, quad_done(q))
                act.wait_ge(s_hbd_lo, quad_done(q - 4))
                act.wait_ge(s_hbd, quad_done(q - 4))
                act.sem_inc(s_seen, 1)
                for values in (hid[:, i], hid_hi[:, i].bitcast(F32R)):
                    ins = act.activation(values, PS[:, 4 + i, 0:NG], ACT.Relu, bias=b1[:, bass.ds(q, 1)])
                ins.then_inc(s_hid, 1)

            def high_weights(k, i):
                act.wait_ge(s_w2[i % 2], slot_done(2 * k + i // 2, 16))
                act.wait_ge(s_y, quad_done(4 * k + i - 4))
                act.sem_inc(s_seen, 1)
                act.activation(w2_hi[:, i], w2[:, i % 2], ACT.Copy).then_inc(s_w2_hi, 1)

            def keep(k, i):
                q = 4 * k + i
                act.wait_ge(s_y, quad_done(q))
                act.activation(PT[:, :, bass.ds(q * J, J), :],
                               two_banks(i % 2).rearrange("p c (j n) -> p c j n", j=J),
                               ACT.Copy).then_inc(s_ye, 1)

            act.wait_ge(s_gat, gathered(NT - 1))
            pipelined(act, NQ, (hidden, 0), (high_weights, 0), (keep, 2), turn=4)

            act.wait_ge(s_choiceT, done(NI - 1))
            with act.Fori(0, NT // 2) as k:
                for s in range(2):
                    t = 2 * k + s
                    act.wait_ge(s_sum, done(t - 2))
                    act.activation(chf[:, s], choiceT[:, bass.ds(t * P, P)], ACT.Copy).then_inc(s_chf, 1)
                    act.wait_ge(s_bp, done(t))
                    act.activation(back[:, s], two_banks(s).rearrange("p b (g d) -> p (b g) d", d=D),
                                   ACT.Copy).then_inc(s_back, 1)

        @block.vector
        def _(dve):
            prime(dve, s_choice3T, s_stat, s_aggr, s_rstd, s_xn, s_lg, s_mx, s_choiceT,
                  s_grp[0], s_xo)
            prime(dve, s_quad, s_hid_lo, s_hbd, s_w2_lo, by=4)
            prime(dve, *s_gathered[1::2], by=1)
            def stats(k, s):
                dve.wait_ge(s_x[s], slot_done(k, 16 * G))
                for t in range(IT):
                    ins = dve.bn_stats(st6[:, s, t], xin[:, 2 * (k % 2) + s, t])
                ins.then_inc(s_stat, 1)

            def variances(k, s):
                dve.wait_ge(s_stat, done(2 * k + s))
                dve.sem_inc(s_seen, 1)
                for t in range(IT):
                    ins = dve.bn_aggr(mv[:, s, t], st6[:, s, t])
                ins.then_inc(s_aggr, 1)

            def invert(k, s):
                dve.wait_ge(s_std, done(2 * k + s))
                dve.reciprocal(rstd[:, s], std[:, s]).then_inc(s_rstd, 1)

            def norm(k, s):
                n = 2 * k + s
                dve.wait_ge(s_rstd, done(n))
                dve.wait_ge(s_tp, done(n - 2))
                dve.wait_ge(s_rest, done(n - 2))
                for t in range(IT):
                    ins = dve.tensor_scalar(xn[:, s, t], xin[:, 2 * (k % 2) + s, t], mv[:, s, t, 0:1],
                                            rstd[:, s, t:t + 1], ALU.subtract, ALU.mult)
                ins.then_inc(s_xn, 1)

            def add(k, s):
                dve.wait_ge(s_lgp, done(2 * k + s))
                dve.scalar_tensor_tensor(
                    lg[:, s], PS[:, 4 + s, :].rearrange("p (g t) -> p g t", t=GT), bc[:, 0:1],
                    tie[:, None, :].broadcast_to([P, IT * G, GT]), ALU.add, ALU.add
                ).then_inc(s_lg, 1)

            def maximum(k, s):
                dve.wait_ge(s_lg, done(2 * k + s))
                dve.tensor_reduce(mx[:, s], lg[:, s], AX.X, ALU.max).then_inc(s_mx, 1)

            def choose(k, s):
                n = 2 * k + s
                dve.wait_ge(s_mx, done(n))
                dve.tensor_tensor(
                    choiceT[:, bass.ds(n * IT * P, IT * P)].rearrange("p (g t) -> p g t", t=GT),
                    lg[:, s], mx[:, s, :, None].broadcast_to([P, IT * G, GT]), ALU.is_equal
                ).then_inc(s_choiceT, 1)

            def three_times(k, s):
                n = 2 * k + s
                dve.wait_ge(s_choiceT, done(n))
                dve.wait_ge(s_turn, choice_turned(IT * (n - 1) - 1))
                dve.sem_inc(s_seen, 1)
                dve.tensor_copy(
                    choice3T[:, s],
                    choiceT[:, bass.ds(n * IT * P, IT * P)].rearrange("p (g t) -> p g t", t=GT)[:, :, None, :]
                    .broadcast_to([P, IT * G, PARTS, GT])).then_inc(s_choice3T, 1)

            pipelined(dve, NI, (norm, 1), (maximum, 3), (stats, 0), (add, 2), (variances, 0), (choose, 3),
                      (invert, 0), (three_times, 3))

            with dve.Fori(0, NT // SL) as k:
                for i in range(1, SL, 2):
                    dve.wait_ge(s_gat, gathered(SL * k + i))
                    dve.tensor_copy(PT[:, :, :, bass.ds((SL * k + i) * G, G)],
                                    two_banks(i).rearrange("p c (g x) -> p c x g", g=G)
                                    ).then_inc(s_gathered[i], 1)

            def take(k, i):
                q = 4 * k + i
                dve.wait_ge(s_h, quad_done(q - 2))
                dve.tensor_copy(quad[:, i % 2].rearrange("p c j n -> p c (j n)"),
                                PT[:, :, bass.ds(q * J, J), :].rearrange("p c j n -> p c (j n)")
                                ).then_inc(s_quad, 1)

            def low_hidden(k, i):
                dve.wait_ge(s_hid, quad_done(4 * k + i))
                dve.tensor_tensor(hid[:, i], hid[:, i], hid_hi[:, i], ALU.subtract).then_inc(s_hid_lo, 1)

            def low_weights(k, i):
                dve.wait_ge(s_w2_hi, quad_done(4 * k + i))
                dve.tensor_tensor(w2_lo[:, i], w2[:, i % 2], w2_hi[:, i].bitcast(F32), ALU.subtract
                                  ).then_inc(s_w2_lo, 1)

            def spread_high(k, i):
                dve.wait_ge(s_y, quad_done(4 * k + i - 2))
                dve.tensor_tensor(hbd[:, i % 2], hid_hi[:, i, None, :].broadcast_to([P, J, NG]),
                                  jmask[:, :, None].broadcast_to([P, J, NG]), ALU.mult
                                  ).then_inc(s_hbd, 1)

            for i in range(SL):
                dve.wait_ge(s_gathered[i], slot_done(NT // SL - 1))
            dve.wait_ge(s_const, ALL_CONST)

            pipelined(dve, NQ, (spread_high, 2), (take, 0), (low_hidden, 1), (low_weights, 1), turn=4)

            def group(k, i):
                t, s = SL * k + i, i % 2
                dve.wait_ge(s_bp, done(t - 2))
                dve.tensor_tensor(
                    grp[:, s, :, 0, :].rearrange("p g x -> p x g"), PT[:, 0, :, bass.ds(t * G, G)],
                    b2[:, 0, :, None].broadcast_to([P, NX, G]), ALU.add).then_inc(s_grp[0], 1)

            def result(k, i):
                dve.wait_ge(s_sum, done(SL * k + i))
                s, half = divmod(i, 2)
                dve.wait_ge(s_xr[s], slot_done(k, 16))
                dve.wait_ge(s_out[s], slot_done(k - 1, 16))
                dve.scalar_tensor_tensor(xo[:, s, half], PS[:, 6 + half, 0:D], 0.5, xr[:, s, half],
                                         ALU.mult, ALU.add).then_inc(s_xo, 1)

            dve.wait_ge(s_ye, quad_done(NQ - 1))
            pipelined(dve, NT, (group, 0), (result, 2), turn=SL)

        @block.tensor
        def _(pe):
            prime(pe, s_turn, by=2 * IT)
            prime(pe, s_tp, s_lgp, s_bp, s_sum)
            prime(pe, s_h, s_y, by=4)
            prime(pe, s_gat, by=SL)
            pe.wait_ge(s_const, CONST)
            pe.wait_ge(s_set, 2)

            def transposes(k, s):
                pe.wait_ge(s_xn, done(2 * k + s))
                pe.wait_ge(s_xT, done(2 * k + s - 2))
                for c in range(C):
                    in_order = PS[:, 2 * s + c, :].rearrange("p (g j t) -> p j t g", g=G, j=IT)
                    for j in range(IT):
                        ins = pe.transpose(in_order[:, j], xn[:, s, j, c * P:(c + 1) * P], idf[:])
                ins.then_inc(s_tp, 1)

            def logits(k, s):
                pe.wait_ge(s_xT, done(2 * k + s))
                pe.wait_ge(s_lg, done(2 * k + s - 2))
                for c in range(C):
                    ins = pe.matmul(PS[:, 4 + s, :], wc[:, c], xT[:, s, c], start=c == 0, stop=c == C - 1)
                ins.then_inc(s_lgp, 1)

            def turns(h):
                def f(k, s):
                    t = IT * (2 * k + s) + h
                    pe.wait_ge(s_choice3T, done(2 * k + s))
                    pe.wait_ge(s_choice, done(t - 2))
                    for g in range(G):
                        ins = pe.matmul(PS[0:PARTS * GT, 6 + h % 2, g * NX:(g + 1) * NX],
                                        choice3T[:, s, h * G + g].rearrange("p k t -> p (k t)"),
                                        idb[:], start=True, stop=True)
                    ins.then_inc(s_turn, 1)
                return f

            pipelined(pe, NI, (transposes, 0), (turns(0), 3), (turns(1), 3), (logits, 0),
                      (turns(2), 3), (turns(3), 3))

            pe.wait_ge(s_choice, done(NT - 1))
            for s in range(2):
                pe.wait_ge(s_parts[s], slot_done(NI // 2 - 1, 16))
            with pe.Fori(0, NT // (GI * SL)) as k8:
                for i8 in range(GI * SL):
                    t, m, i = GI * SL * k8 + i8, i8 // GI, i8 % SL
                    if i8 % GI == 0:
                        pe.wait_ge(s_stack[m], slot_done(k8, 16))
                    pe.wait_ge(s_gathered[i], slot_done(GI * k8 + i8 // SL - 1))
                    for c in range(C):
                        for g in range(G):
                            ins = pe.matmul(PS[:, 2 * i + c, g * NX:(g + 1) * NX],
                                            stack[:, m, i8 % GI * G + g, c * P:(c + 1) * P],
                                            choice[:, t * G + g, :], start=True, stop=True)
                    ins.then_inc(s_gat, 1)

            def first_product(k, i):
                pe.wait_ge(s_quad, quad_done(4 * k + i))
                pe.wait_ge(s_w1[i % 2], slot_done(2 * k + i // 2, 16))
                pe.wait_ge(s_hid, quad_done(4 * k + i - 4))
                for c in range(C):
                    for j in range(J):
                        ins = pe.matmul(PS[j * F:(j + 1) * F, 4 + i, 0:NG],
                                        w1[:, i % 2, c, j * F:(j + 1) * F], quad[:, i % 2, c, j],
                                        start=c == 0, stop=c == C - 1)
                ins.then_inc(s_h, 1)

            def second_product(k, i):
                q, s = 4 * k + i, i % 2
                pe.wait_ge(s_hbd, quad_done(q))
                pe.wait_ge(s_hbd_lo, quad_done(q))
                pe.wait_ge(s_w2_lo, quad_done(q))
                pe.wait_ge(s_ye, quad_done(q - 2))
                high, low = (h[:, i % 2].rearrange("p j n -> p (j n)") for h in (hbd, hbd_lo))
                for c in range(C):
                    w_high, w_low = (w[:, i, c * P:(c + 1) * P] for w in (w2_hi, w2_lo))
                    pe.matmul(PS[:, 2 * s + c, :], w_high, high, start=True, stop=False)
                    pe.matmul(PS[:, 2 * s + c, :], w_high, low, start=False, stop=False)
                    ins = pe.matmul(PS[:, 2 * s + c, :], w_low, high, start=False, stop=True)
                ins.then_inc(s_y, 1)

            for i in range(SL):
                pe.wait_ge(s_gathered[i], slot_done(NT // SL - 1))
            pipelined(pe, NQ, (first_product, 0), (second_product, 2), turn=4)

            def by_expert(k, s):
                for c in range(C):
                    pe.wait_ge(s_grp[c], done(2 * k + s))
                pe.wait_ge(s_back, done(2 * k + s - 2))
                for g in range(G):
                    for c in range(C):
                        at = (g % 2) * D + c * P
                        ins = pe.transpose(PS[:, 2 * s + g // 2, at:at + P], grp[:, s, g, c], idf[:])
                ins.then_inc(s_bp, 1)

            def to_tokens(k, s):
                pe.wait_ge(s_back, done(2 * k + s))
                pe.wait_ge(s_chf, done(2 * k + s))
                pe.wait_ge(s_xo, done(2 * k + s - 2))
                for g in range(G):
                    ins = pe.matmul(PS[g * GT:(g + 1) * GT, 6 + s, 0:D], chf[:, s, g * GT:(g + 1) * GT],
                                    back[:, s, g], start=True, stop=True)
                ins.then_inc(s_sum, 1)

            pipelined(pe, NT, (by_expert, 0), (to_tokens, 1))


def attention_stage(nc, src, dst, wts, s_seen):
    qk_d = nc.dram_tensor("qk_parts", (QK, DIL, C, 2, PARTS, P, BANK), BF16).ap()
    qk_units = qk_d.rearrange("a i c f r p m -> a (i c) f p r m")
    qk_rows = qk_d.rearrange("a i c f r (d h) m -> a c i f (r d) (h m)", d=HD)
    by_batch = src.rearrange("(b m i) d -> b m i d", b=BATCH, i=DIL)
    src_tiles = src.rearrange("(b m i) d -> i b m d", b=BATCH, i=DIL)
    dst_tiles = dst.rearrange("(b m i) d -> i b m d", b=BATCH, i=DIL)

    with ExitStack() as ctx:
        def sb(name, shape, dt=F32):
            return ctx.enter_context(nc.sbuf_tensor(f"{name}_at", shape, dt))

        def sem(name):
            return nc.alloc_semaphore(f"{name}_at")

        def sems(name, n=2):
            return [sem(f"{name}{s}_") for s in range(n)]

        xnT = sb("xnT", [P, C, DIL, BATCH, P])
        stack = sb("stack", [PAIRS * HD, 2, QK, C, HC, BANK], BF16)
        tiles = "p c i b m -> p c (i b) m"
        xin = sb("xin", [P, 4, DIL, D])
        split = xin[:].rearrange("p s i d -> p (s i d)").bitcast(BF16)[:, 0:4 * PARTS * BANK].rearrange(
            "p (u r m) -> p u r m", u=4, r=PARTS)
        xn = sb("xn", [P, 2, DIL, D])
        y = xn[:].rearrange("p s i d -> p (s i d)").rearrange("p (u m) -> p u m", u=4)
        st6 = sb("st6", [P, 2, DIL, 6])
        mv = sb("mv", [P, 2, DIL, 2])
        eps = sb("eps", [P, 1])
        std = sb("std", [P, 2, DIL])
        rstd = sb("rstd", [P, 2, DIL])
        idf = sb("idf", [P, P])
        wqk = sb("wqk", [P, 2, C, 2 * D])
        wv = sb("wv", [P, DIL, C, D])
        wo = sb("wo", [P, DIL, C, D])
        bqk = sb("bqk", [P, QK, DIL * C])
        bv = sb("bv", [P, DIL, D])
        bo = sb("bo", [P, DIL, D])
        prob = sb("prob", [P, 2, NB, HB, P])
        probT = sb("probT", [P, 2, NB, HB, P])
        low = sb("low", [P, 2, H])
        total = sb("total", [P, 2, H])
        scale = sb("scale", [P, 2, H])
        scale_wide = sb("scale_wide", [P, 2, D])
        scaleT = sb("scaleT", [P, D])
        xs = sb("xs", [P, 2, C, P])
        v = sb("v", [P, 2, H, 2 * HD])
        oT = sb("oT", [P, 2, D])
        xr = sb("xr", [P, 2, D])
        xrb = sb("xrb", [P, 2, D])
        xo = sb("xo", [P, 2, D])
        PS = ctx.enter_context(nc.psum_tensor("PS_at", [P, 8, BANK], F32))
        TURN, OUTB, MISC = NB, NB + 2, NB + 3

        s_const, s_set, s_x = sem("const"), sem("set"), sems("x")
        s_stat, s_aggr, s_std, s_rstd, s_xn, s_tp, s_xT = (
            sem("stat"), sem("aggr"), sem("std"), sem("rstd"), sem("xn"), sem("tp"), sem("xT"))
        s_wqk, s_p, s_hi, s_rest, s_mid, s_lo, s_split = (
            sems("wqk"), sem("p"), sem("hi"), sem("rest"), sem("mid"), sem("lo"), sems("split", 4))
        s_load, s_stacked = sems("load"), sem("stacked")
        s_s, s_low, s_exp, s_turn, s_pT = (
            sem("s"), sem("low"), sem("exp"), sem("turn"), sems("pT"))
        s_xs, s_vp, s_v, s_scale, s_wide, s_wideT, s_scaleT, s_pv, s_oT = (
            sem("xs"), sem("vp"), sem("v"), sem("scale"), sem("wide"), sem("wideT"), sem("scaleT"),
            sem("pv"), sem("oT"))
        s_proj, s_xr, s_xrb, s_xo, s_out = sem("proj"), sems("xr"), sem("xrb"), sem("xo"), sems("out")

        consts = [(idf, wts["idf"]), (bqk, wts["bqk"])]
        late_consts = [(wv, wts["wv"]), (wo, wts["wo"]), (bv, wts["bv"]), (bo, wts["bo"])]
        CONST = 16 * len(consts)
        ALL_CONST = CONST + 16 * len(late_consts)

        def bank_done(u):
            return u + 1 + 2 * NB

        def unit_done(u):
            return u + 1 + 4

        block = ctx.enter_context(nc.Block())

        @block.sync
        def _(sp):
            prime(sp, *s_x, *s_wqk, *s_split, *s_xr, *s_out, by=16)
            prime(sp, *s_load, by=16 * QK * C * PARTS)

            def load_x(k, s):
                sp.wait_ge(s_stat, done(2 * k + s - 2))
                sp.dma_start(xin[:, 2 * (k % 2) + s], by_batch[2 * k + s]).then_inc(s_x[s], 16)

            load_x(0, 0)
            load_x(0, 1)
            for a, b in consts:
                sp.dma_start(a[:], b).then_inc(s_const, 16)
            with sp.Fori(1, BATCH // 2) as k:
                for s in range(2):
                    load_x(k, s)
            for s in range(2):
                sp.dma_start(wqk[:, s], wts["wqk"][s]).then_inc(s_wqk[s], 16)
            sp.wait_ge(s_const, CONST)
            for a, b in late_consts:
                sp.dma_start(a[:], b).then_inc(s_const, 16)
            def store_split(k):
                for i in range(4):
                    f, a = divmod(i, 2)
                    sp.wait_ge(s_lo, done(4 * k + i))
                    sp.dma_start(qk_units[a, k, f], split[:, i]).then_inc(s_split[i], 16)

            def load_group(a, c, i, f):
                at = 0
                for n in range(PARTS, 0, -1):
                    first = (PARTS - n) * a
                    sp.dma_start(
                        stack[at * HD:(at + n) * HD, f, a, c].rearrange("p h m -> p (h m)"),
                        qk_rows[a, c, i, f, first * HD:(first + n) * HD, :]).then_inc(s_load[f], 16)
                    at += n

            def announce(k, f):
                sp.wait_ge(s_load[f], slot_done(k, 16 * QK * C * PARTS))
                sp.sem_inc(s_stacked, 1)

            groups = [(a, c) for a in range(QK) for c in range(C)]
            with sp.Fori(0, 2) as k:
                store_split(k)
            for i in range(2):
                sp.wait_ge(s_p, done(8 * i + 7))
                sp.dma_start(wqk[:, i], wts["wqk"][2 + i]).then_inc(s_wqk[i], 16)
                for c in range(C):
                    store_split(2 + 2 * i + c)
                    for a in range(QK if i == c == 0 else 0):
                        sp.wait_ge(s_split[a], slot_done(1, 16))
                    load_group(*groups[2 * i + c], 0, 0)
            store_split(6)
            announce(0, 0)
            store_split(7)
            for a in range(QK):
                sp.wait_ge(s_split[2 + a], slot_done(1, 16))
            for g in range(4):
                load_group(*groups[g], 0, 1)
            for i in range(4):
                sp.wait_ge(s_split[i], slot_done(7, 16))

            def load_xr(t, s, branch, b):
                sp.wait_ge(s_xrb, done(t - 2))
                sp.dma_start(xr[:, s], src_tiles[branch, b]).then_inc(s_xr[s], 16)

            def store_xo(t, s, branch, b):
                sp.wait_ge(s_xo, done(t))
                sp.dma_start(dst_tiles[branch, b], xo[:, s]).then_inc(s_out[s], 16)

            def rows(k, i):
                if not (isinstance(k, int) and k == 0 and i < 3):
                    j = i - 3
                    store_xo(8 * k + j, j % 2, k + j // 8, j % 8)
                if not (isinstance(k, int) and 8 * k + i >= NT):
                    load_xr(8 * k + i, i % 2, k + i // 8, i % 8)

            for i in range(4):
                rows(0, i)
            announce(0, 1)
            with sp.Fori(0, NT // 8 - 1) as k:
                for f in range(2):
                    for j in range(4):
                        if j == 0:
                            sp.wait_ge(s_s, bank_done(NB * (8 * k + 4 * f + 3) + NB - 1))
                        load_group(*groups[j], k + 1, f)
                        rows(k, 4 + 4 * f + j)
                    announce(k + 1, f)
            for i in range(4, 8 + 3):
                rows(NT // 8 - 1, i)
            for s in range(2):
                sp.wait_ge(s_out[s], slot_done(NT // 2 - 1, 16))

        @block.gpsimd
        def _(pool):
            prime(pool, s_lo, s_xs, s_xrb)
            pool.memset(eps[:], EPS).then_inc(s_set, 1)
            pool.memset(v[:], 0.0).then_inc(s_set, 1)
            pool.wait_ge(s_const, CONST)
            pool.tensor_scalar(bqk[:, 0], bqk[:, 0], -float(HD) ** -0.5, None, ALU.mult).then_inc(s_set, 1)

            pool.wait_ge(s_const, ALL_CONST)
            pool.tensor_scalar(bo[:], bo[:], BRANCH_WEIGHT, None, ALU.mult).then_inc(s_set, 1)
            pool.wait_ge(s_set, 4)

            def low_part(k, i):
                pool.wait_ge(s_mid, done(4 * k + i))
                pool.tensor_tensor(split[:, i, (PARTS - 1) * (1 - i % 2)], y[:, i], split[:, i, 1],
                                   ALU.subtract).then_inc(s_lo, 1)

            pipelined(pool, 8 * DIL, (low_part, 0), turn=4)

            x_tiles = xnT[:].rearrange(tiles)

            def tile_columns(k, s):
                pool.wait_ge(s_vp, done(2 * k + s - 2))
                pool.sem_inc(s_seen, 1)
                pool.tensor_copy(xs[:, s], x_tiles[:, :, 2 * k + s, :]).then_inc(s_xs, 1)

            def residual(k, s):
                pool.wait_ge(s_xr[s], slot_done(k, 16))
                pool.wait_ge(s_xo, done(2 * k + s - 2))
                pool.sem_inc(s_seen, 1)
                pool.tensor_tensor(xrb[:, s], xr[:, s], bo[:, k // 4], ALU.add).then_inc(s_xrb, 1)

            pipelined(pool, NT, (tile_columns, 0), (residual, 2))

        @block.scalar
        def _(act):
            prime(act, s_std, s_xT)
            prime(act, s_hi, by=4)
            prime(act, s_exp, by=2 * NB)
            prime(act, s_pT[1], by=1)
            act.wait_ge(s_set, 2)

            def deviations(k, s):
                act.wait_ge(s_aggr, done(2 * k + s))
                act.wait_ge(s_rstd, done(2 * k + s - 2))
                act.activation(std[:, s], mv[:, s, :, 1], ACT.Sqrt, bias=eps[:, 0:1]
                               ).then_inc(s_std, 1)

            def columns(k, s):
                act.wait_ge(s_tp, done(2 * k + s))
                act.activation(xnT[:, :, :, 2 * k + s, :],
                               PS[:, 2 * s:2 * s + 2, :].rearrange("p c (i m) -> p c i m", i=DIL),
                               ACT.Copy).then_inc(s_xT, 1)

            pipelined(act, BATCH, (deviations, 0), (columns, 2))

            act.wait_ge(s_const, CONST)
            act.wait_ge(s_set, 3)

            def values(k, i):
                a = i % 2
                act.wait_ge(s_p, done(4 * k + i))
                act.wait_ge(s_split[i], slot_done(k - 1, 16))
                act.sem_inc(s_seen, 1)
                for result in (y[:, i], split[:, i, (PARTS - 1) * a]):
                    ins = act.activation(result, PS[:, 4 + i, :], ACT.Identity, bias=bqk[:, a, bass.ds(k, 1)],
                                         scale=1.0 if a else -float(HD) ** -0.5)
                ins.then_inc(s_hi, 1)

            pipelined(act, 8 * DIL, (values, 0), turn=4)

            def exps(j):
                def f(k, s):
                    u = NB * (2 * k + s) + j
                    act.wait_ge(s_low, bank_done(u))
                    act.wait_ge(s_turn, bank_done(u - 2 * NB))
                    act.wait_ge(s_scale, done(2 * k + s - 2))
                    for g in range(HB):
                        h = HB * j + g
                        ins = act.activation(prob[:, s, j, g], PS[:, j, g * P:(g + 1) * P], ACT.Exp,
                                             bias=low[:, s, h:h + 1], scale=-1.0,
                                             accum_out=total[:, s, h:h + 1])
                    ins.then_inc(s_exp, 1)
                return f

            def turned(j):
                def f(k, s):
                    act.wait_ge(s_turn, bank_done(NB * (2 * k + s) + j))
                    act.activation(probT[:, s, j].rearrange("p g q -> p (g q)"), PS[:, TURN + 1, :],
                                   ACT.Copy).then_inc(s_pT[1], 1)
                return f

            pipelined(act, NT, (exps(0), 0), (turned(1), 1), (exps(1), 0),
                      (exps(2), 0), (turned(3), 1), (exps(3), 0))

        @block.vector
        def _(dve):
            prime(dve, s_stat, s_aggr, s_rstd, s_xn, s_rest, s_mid, s_v, s_scale, s_wide, s_scaleT, s_oT, s_xo)
            prime(dve, s_low, by=2 * NB)
            prime(dve, s_pT[0], by=1)

            def stats(k, s):
                dve.wait_ge(s_x[s], slot_done(k, 16))
                for t in range(DIL):
                    ins = dve.bn_stats(st6[:, s, t], xin[:, 2 * (k % 2) + s, t])
                ins.then_inc(s_stat, 1)

            def invert(k, s):
                dve.wait_ge(s_std, done(2 * k + s))
                dve.reciprocal(rstd[:, s], std[:, s]).then_inc(s_rstd, 1)

            def variances(k, s):
                dve.wait_ge(s_stat, done(2 * k + s))
                dve.sem_inc(s_seen, 1)
                for t in range(DIL):
                    ins = dve.bn_aggr(mv[:, s, t], st6[:, s, t])
                ins.then_inc(s_aggr, 1)

            def norm(k, s):
                n = 2 * k + s
                dve.wait_ge(s_rstd, done(n))
                dve.wait_ge(s_tp, done(n - 2))
                for t in range(DIL):
                    ins = dve.tensor_scalar(xn[:, s, t], xin[:, 2 * (k % 2) + s, t], mv[:, s, t, 0:1],
                                            rstd[:, s, t:t + 1], ALU.subtract, ALU.mult)
                ins.then_inc(s_xn, 1)

            pipelined(dve, BATCH, (stats, 0), (invert, 1), (variances, 0), (norm, 1))

            def rest(k, i):
                dve.wait_ge(s_hi, unit_done(4 * k + i))
                dve.tensor_tensor(y[:, i], y[:, i], split[:, i, (PARTS - 1) * (i % 2)], ALU.subtract
                                  ).then_inc(s_rest, 1)

            def middle(k, i):
                dve.wait_ge(s_rest, done(4 * k + i))
                dve.tensor_copy(split[:, i, 1], y[:, i]).then_inc(s_mid, 1)

            pipelined(dve, 8 * DIL, (rest, 0), (middle, 0), turn=4)

            def lows(j):
                def f(k, s):
                    u = NB * (2 * k + s) + j
                    dve.wait_ge(s_s, bank_done(u))
                    dve.wait_ge(s_exp, bank_done(u - 2 * NB))
                    dve.tensor_reduce(low[:, s, HB * j:HB * (j + 1)],
                                      PS[:, j, :].rearrange("p (g k) -> p g k", g=HB), AX.X, ALU.min
                                      ).then_inc(s_low, 1)
                return f

            def turned(j):
                def f(k, s):
                    dve.wait_ge(s_turn, bank_done(NB * (2 * k + s) + j))
                    dve.tensor_copy(probT[:, s, j].rearrange("p g q -> p (g q)"), PS[:, TURN, :]
                                    ).then_inc(s_pT[0], 1)
                return f

            def scales(k, s):
                n = 2 * k + s
                dve.wait_ge(s_exp, bank_done(NB * n + NB - 1))
                dve.wait_ge(s_wide, done(n - 2))
                dve.reciprocal(scale[:, s], total[:, s]).then_inc(s_scale, 1)
                dve.wait_ge(s_scale, done(n))
                dve.wait_ge(s_wideT, done(n - 2))
                dve.tensor_copy(scale_wide[:, s].rearrange("p (h d) -> p h d", h=H),
                                scale[:, s, :, None].broadcast_to([P, H, HD])).then_inc(s_wide, 1)

            def values(k, s):
                dve.wait_ge(s_vp, done(2 * k + s))
                dve.wait_ge(s_pv, done(2 * k + s - 2))
                for o in range(2):
                    odd = "p (h o d) -> p h o d"
                    ins = dve.tensor_tensor(
                        v[:, s].rearrange("p (h o) d -> p h o d", o=2)[:, :, o, o * HD:(o + 1) * HD],
                        PS[:, MISC, 0:D].rearrange(odd, o=2, d=HD)[:, :, o],
                        bv[:, k // 4].rearrange(odd, o=2, d=HD)[:, :, o], ALU.add)
                ins.then_inc(s_v, 1)

            def scaled(k, s):
                n = 2 * k + s
                dve.wait_ge(s_wideT, done(n))
                dve.wait_ge(s_oT, done(n - 1))
                dve.tensor_copy(scaleT[:], PS[:, OUTB, D:2 * D]).then_inc(s_scaleT, 1)
                dve.wait_ge(s_scaleT, done(n))
                dve.wait_ge(s_proj, done(n - 2))
                dve.tensor_tensor(oT[:, s], PS[:, OUTB, 0:D], scaleT[:], ALU.mult).then_inc(s_oT, 1)

            def result(k, s):
                dve.wait_ge(s_proj, done(2 * k + s))
                dve.wait_ge(s_xrb, done(2 * k + s))
                dve.wait_ge(s_out[s], slot_done(k - 1, 16))
                dve.scalar_tensor_tensor(xo[:, s], PS[:, MISC, D:2 * D], BRANCH_WEIGHT, xrb[:, s],
                                         ALU.mult, ALU.add).then_inc(s_xo, 1)

            dve.wait_ge(s_set, 2)
            dve.wait_ge(s_const, ALL_CONST)
            pipelined(dve, NT, (lows(0), 0), (turned(0), 1), (lows(1), 0), (scales, 1), (scaled, 2),
                      (lows(2), 0), (turned(2), 1), (result, 2), (lows(3), 0), (values, 0))

        @block.tensor
        def _(pe):
            prime(pe, s_tp, s_p, s_vp, s_wideT, s_pv, s_proj)
            prime(pe, s_s, s_turn, by=2 * NB)
            pe.wait_ge(s_const, CONST)

            with pe.Fori(0, BATCH // 2) as k:
                for s in range(2):
                    n = 2 * k + s
                    pe.wait_ge(s_xn, done(n))
                    pe.wait_ge(s_xT, done(n - 2))
                    for c in range(C):
                        for i in range(DIL):
                            ins = pe.transpose(PS[:, 2 * s + c, i * P:(i + 1) * P],
                                               xn[:, s, i, c * P:(c + 1) * P], idf[:])
                    ins.then_inc(s_tp, 1)

            pe.wait_ge(s_xT, done(BATCH - 1))
            with pe.Fori(0, DIL // 2) as k:
                for s in range(2):
                    i = 2 * k + s
                    pe.wait_ge(s_wqk[s], slot_done(k, 16))
                    for c in range(C):
                        for h in range(2):
                            for a in range(QK):
                                unit, bank = 8 * i + 4 * c + 2 * h + a, 4 + 2 * h + a
                                pe.wait_ge(s_hi, unit_done(unit - 4))
                                at = a * D + c * P
                                for e in range(C):
                                    ins = pe.matmul(
                                        PS[:, bank, :], wqk[:, s, e, at:at + P],
                                        xnT[:, e, i, h * HALF:(h + 1) * HALF].rearrange("p b m -> p (b m)"),
                                        start=e == 0, stop=e == C - 1)
                                ins.then_inc(s_p, 1)
            pe.wait_ge(s_hi, unit_done(8 * DIL - 1))

            def scores(j):
                def f(k, s):
                    t = 2 * k + s
                    pe.wait_ge(s_stacked, k // 2 + 1)
                    pe.wait_ge(s_exp, bank_done(NB * (t - 1) + j))
                    at = (k % 2 * 2 + s) * P
                    for g in range(HB):
                        h = HB * j + g
                        ins = pe.matmul(PS[:, j, g * P:(g + 1) * P],
                                        stack[:, k // 2 % 2, 0, h // HC, h % HC, bass.ds(at, P)],
                                        stack[:, k // 2 % 2, 1, h // HC, h % HC, bass.ds(at, P)],
                                        start=True, stop=True)
                    ins.then_inc(s_s, 1)
                return f

            def turns(j):
                def f(k, s):
                    t = 2 * k + s
                    pe.wait_ge(s_exp, bank_done(NB * t + j))
                    pe.wait_ge(s_pT[j % 2], slot_done(2 * t + j // 2 - 1))
                    for g in range(HB):
                        ins = pe.transpose(PS[:, TURN + j % 2, g * P:(g + 1) * P], prob[:, s, j, g], idf[:])
                    ins.then_inc(s_turn, 1)
                return f

            def values(k, s):
                pe.wait_ge(s_xs, done(2 * k + s))
                pe.wait_ge(s_xo, done(2 * k + s - 2))
                for e in range(C):
                    ins = pe.matmul(PS[:, MISC, 0:D], xs[:, s, e], wv[:, k // 4, e], start=e == 0,
                                    stop=e == C - 1)
                ins.then_inc(s_vp, 1)

            def weighted(k, s):
                t = 2 * k + s
                pe.wait_ge(s_v, done(t))
                for o in range(2):
                    pe.wait_ge(s_pT[o], slot_done(2 * t + 1))
                pe.wait_ge(s_oT, done(t - 1))
                for c in range(C):
                    for o in range(2):
                        for r in range(HC // 2):
                            h = c * HC + 2 * r + o
                            ins = pe.matmul(PS[r * 2 * HD:(r + 1) * 2 * HD, OUTB, c * P:(c + 1) * P],
                                            v[:, s, h], probT[:, s, h // HB, h % HB], start=o == 0, stop=o == 1)
                ins.then_inc(s_pv, 1)

            def scale_rows(k, s):
                pe.wait_ge(s_wide, done(2 * k + s))
                for c in range(C):
                    ins = pe.transpose(PS[:, OUTB, D + c * P:D + (c + 1) * P],
                                       scale_wide[:, s, c * P:(c + 1) * P], idf[:])
                ins.then_inc(s_wideT, 1)

            def project(k, s):
                pe.wait_ge(s_oT, done(2 * k + s))
                t = 2 * k + s
                pe.wait_ge(s_v, done(min(t + 1, NT - 1) if isinstance(k, int) else t + 1))
                for c in range(C):
                    ins = pe.matmul(PS[:, MISC, D:2 * D], oT[:, s, c * P:(c + 1) * P], wo[:, k // 4, c],
                                    start=c == 0, stop=c == C - 1)
                ins.then_inc(s_proj, 1)

            pe.wait_ge(s_const, ALL_CONST)
            pipelined(pe, NT, (scores(0), 0), (turns(0), 1), (scores(1), 0), (turns(1), 1), (weighted, 2),
                      (scale_rows, 2), (scores(2), 0), (turns(2), 1), (project, 2), (scores(3), 0),
                      (turns(3), 1), (values, 0))


def macaron(nc, x, out, wts):
    x1 = nc.dram_tensor("x1", (TOK, D), F32).ap()
    x2 = nc.dram_tensor("x2", (TOK, D), F32).ap()
    with nc.semaphore("seen") as s_seen:
        with nc.cleanup_on_exit():
            ffn_stage(nc, "a", x, x1, wts, s_seen)
        with nc.cleanup_on_exit():
            attention_stage(nc, x1, x2, wts, s_seen)
        ffn_stage(nc, "b", x2, out, wts, s_seen)


_INS = ["x", "wc", "bc", "tie", "w1", "b1", "w2", "b2", "idf", "jmask", "wqk", "bqk", "wv", "bv",
        "wo", "bo"]


def kernel(L0_attn_x, L0_attn_Wqkv, L0_attn_bqkv, L0_attn_Wo, L0_attn_bo,
           L0_ffn_Wc, L0_ffn_bc, L0_ffn_W1, L0_ffn_b1, L0_ffn_W2, L0_ffn_b2):
    import concourse.bacc as bacc
    from concourse.bass_utils import run_bass_kernel_spmd

    a = {k: np.asarray(v) for k, v in locals().items() if k.startswith("L0_")}
    f32 = np.float32
    wqkv = a["L0_attn_Wqkv"].reshape(DIL, 3 * D, C, P).transpose(0, 3, 2, 1)
    bqkv = a["L0_attn_bqkv"]
    arrays = {
        "x": a["L0_attn_x"].reshape(TOK, D),
        "wc": a["L0_ffn_Wc"].reshape(C, P, NX).transpose(1, 0, 2),
        "bc": a["L0_ffn_bc"].reshape(NX, 1),
        "tie": np.broadcast_to(np.linspace(0.0, 1e-6, GT, dtype=f32), (P, GT)),
        "w1": a["L0_ffn_W1"].reshape(NQ, J, C, P, F).transpose(0, 3, 2, 1, 4).reshape(NQ, P, C, P),
        "b1": a["L0_ffn_b1"].reshape(NQ, P).T,
        "w2": a["L0_ffn_W2"].reshape(NQ, J, D, F).transpose(0, 1, 3, 2).reshape(NQ, P, D),
        "b2": a["L0_ffn_b2"].reshape(NX, C, P).transpose(2, 1, 0),
        "idf": np.eye(P, dtype=f32),
        "jmask": np.kron(np.eye(J, dtype=f32), np.ones((F, 1), f32)),
        "wqk": wqkv[..., :2 * D].reshape(DIL, P, C, QK * C, HC, HD).swapaxes(-1, -2)
                                .reshape(DIL, P, C, QK * D),
        "bqk": bqkv[:, :2 * D].reshape(DIL, QK, C, HC, HD).transpose(4, 3, 1, 0, 2)
                              .reshape(P, QK, DIL * C),
        "wv": wqkv[..., 2 * D:].transpose(1, 0, 2, 3),
        "bv": np.broadcast_to(bqkv[None, :, 2 * D:], (P, DIL, D)),
        "wo": a["L0_attn_Wo"].reshape(DIL, D, C, P).transpose(3, 0, 2, 1),
        "bo": np.broadcast_to(a["L0_attn_bo"][None], (P, DIL, D)),
    }
    arrays = {f"in_{k}": np.ascontiguousarray(v) for k, v in arrays.items()}
    nc = bacc.Bacc("TRN2", target_bir_lowering=False, num_devices=1)
    aps = {k: nc.dram_tensor(f"in_{k}", arrays[f"in_{k}"].shape, F32, kind="ExternalInput").ap()
           for k in _INS}
    out = nc.dram_tensor("out", (TOK, D), F32, kind="ExternalOutput").ap()
    macaron(nc, aps.pop("x"), out, aps)
    r = run_bass_kernel_spmd(nc, [arrays], core_ids=[0])
    return np.asarray(r.results[0]["out"]).reshape(BATCH, TOK // BATCH, D)
```
